# Optimizing a Trainium2 kernel written in Bass

```python
import numpy as np
import jax
import jax.numpy as jnp

def _softmax(x, axis=-1):
    return jax.nn.softmax(x, axis=axis)

def _gelu(x):
    return jax.nn.gelu(x, approximate=True)

def _silu(x):
    return jax.nn.silu(x)

def _sigmoid(x):
    return jax.nn.sigmoid(x)

def _layernorm(x, axis=-1, eps=1e-05):
    m = jnp.mean(x, axis=axis, keepdims=True)
    v = jnp.var(x, axis=axis, keepdims=True)
    return (x - m) / jnp.sqrt(v + eps)

def _scatter_add(tgt, idx, src, axis=0):
    return tgt.at[idx].add(src)

def _segment_sum(src, seg, n):
    return jax.ops.segment_sum(src, seg, n)
kernel_name = 'mk_adaln_ffn_d1_seqx_r4_611d1b'

def setup_inputs(seed: int=0):
    np.random.seed(seed)
    _w = jnp.asarray

    def _rec_inputs():
        import jax
        import jax.numpy as jnp
        _rk = jax.random.key(seed)
        x = -7.109e-05 + 0.9999 * jax.random.normal(jax.random.fold_in(_rk, 1), (64, 64, 1024), jnp.float32)
        _lenS = 64 - jax.random.randint(jax.random.fold_in(_rk, 7), (64,), 0, max(1, 64 // 4) + 1, jnp.int32)
        _lenS2 = 64 - jax.random.randint(jax.random.fold_in(_rk, 8), (64,), 0, max(1, 64 // 4) + 1, jnp.int32)
        itok_B_0_15 = jax.random.randint(jax.random.fold_in(_rk, 11), (64,), 0, 16, jnp.int32)
        return (x, itok_B_0_15)
    x, itok_B_0_15 = _rec_inputs()

    def _L0_cond_setup():
        import jax, jax.numpy as jnp
        import numpy as np
        NUM_CONDITIONS = 16
        IN_CH = 64
        OUT_CH = 64
        B = 64
        T = 1024
        key = jax.random.key(seed)
        k_x, k_w, k_c = jax.random.split(key, 3)
        x = jax.random.normal(k_x, (B, IN_CH, T), dtype=jnp.float32)
        bound = float(np.sqrt(6.0 / IN_CH))
        weights = jax.random.uniform(k_w, (NUM_CONDITIONS, IN_CH, OUT_CH), dtype=jnp.float32, minval=-bound, maxval=bound)
        condition = jax.random.randint(k_c, (B,), 0, NUM_CONDITIONS, dtype=jnp.int64)
        return {'x': x, 'weights': weights, 'condition': condition}
    _L0_cond_all = _L0_cond_setup()
    _L0_cond_in = {k: v for k, v in _L0_cond_all.items() if k in ('weights',)}
    del _L0_cond_all

    def _L0_ffn_setup():
        import jax, jax.numpy as jnp
        import numpy as np
        TOP_K = 2
        key = jax.random.key(seed)
        k0, k1, k2 = jax.random.split(key, 3)
        B, S, D, H, E = (4, 512, 1024, 1024, 8)
        sc = 1.0 / np.sqrt(D).astype(np.float32)
        x = jax.random.normal(k0, (B, S, D), dtype=jnp.float32)
        W_gate = jax.random.normal(k1, (D, E), dtype=jnp.float32) * sc
        b_gate = jnp.zeros((E,), dtype=jnp.float32)
        W_e = jax.random.normal(k2, (E, D, H), dtype=jnp.float32) * sc
        b_e = jnp.zeros((E, H), dtype=jnp.float32)
        return {'x': x, 'W_gate': W_gate, 'b_gate': b_gate, 'W_e': W_e, 'b_e': b_e}
    _L0_ffn_all = _L0_ffn_setup()
    _L0_ffn_in = {k: v for k, v in _L0_ffn_all.items() if k in ('W_gate', 'b_gate', 'W_e', 'b_e')}
    del _L0_ffn_all
    return {'x': x, 'itok_B_0_15': itok_B_0_15, 'L0_cond_weights': _L0_cond_in['weights'], 'L0_ffn_W_gate': _L0_ffn_in['W_gate'], 'L0_ffn_b_gate': _L0_ffn_in['b_gate'], 'L0_ffn_W_e': _L0_ffn_in['W_e'], 'L0_ffn_b_e': _L0_ffn_in['b_e']}

def reference(x, itok_B_0_15, L0_cond_weights, L0_ffn_W_gate, L0_ffn_b_gate, L0_ffn_W_e, L0_ffn_b_e):
    import jax
    import jax.numpy as jnp

    def _L0_cond_ref(x, weights, condition):
        import jax, jax.numpy as jnp
        import numpy as np
        NUM_CONDITIONS = 16
        IN_CH = 64
        OUT_CH = 64
        B = 64
        T = 1024
        W = weights[condition]
        return jnp.einsum('bct,bcd->bdt', x, W)

    def _L0_ffn_ref(x, W_gate, b_gate, W_e, b_e):
        import jax, jax.numpy as jnp
        import numpy as np
        TOP_K = 2
        logits = x @ W_gate + b_gate
        _, top_idx = jax.lax.top_k(logits, TOP_K)
        y_all = jax.nn.relu(jnp.einsum('bsd,edh->bseh', x, W_e) + b_e)
        y = jnp.take_along_axis(y_all, top_idx[..., None], axis=2)
        return y.mean(axis=2)
    x = x + _L0_ffn_ref(_L0_cond_ref(x, L0_cond_weights, itok_B_0_15), L0_ffn_W_gate, L0_ffn_b_gate, L0_ffn_W_e, L0_ffn_b_e)
    return x

_drawn_inputs = setup_inputs


def setup_inputs(seed=0):
    import zlib

    import numpy as np

    out = dict(_drawn_inputs(seed))
    spreads = {'L0_ffn_b_gate': (0.0, 0.1), 'L0_ffn_b_e': (0.0, 0.1)}
    factors = {}
    for name, (base, spread) in spreads.items():
        noise = np.random.default_rng([zlib.crc32(name.encode()), seed]).standard_normal(out[name].shape)
        drawn = base * np.exp(spread * noise) if base else spread * noise
        out[name] = jnp.asarray(drawn.astype(out[name].dtype))
    for name, factor in factors.items():
        out[name] = (out[name] * factor).astype(out[name].dtype)
    return out
```

```python
from contextlib import ExitStack

import numpy as np
import concourse.bass as bass
from concourse import mybir
from concourse.alu_op_type import AluOpType as ALU

P = 128
F32, F32R, BF16 = mybir.dt.float32, mybir.dt.float32r, mybir.dt.bfloat16
I32, U32 = mybir.dt.int32, mybir.dt.uint32
ACTF = mybir.ActivationFunctionType
AX = mybir.AxisListType
BANK = 512


class Chain:

    def __init__(self, eng, sem):
        self.eng, self.sem, self.base, self.n = eng, sem, 0, 0

    def turn(self, base):
        self.base, self.n = base, 0

    def __call__(self, ins):
        self.n += 1
        ins.then_inc(self.sem, 1)
        self.eng.wait_ge(self.sem, self.base + self.n)


def build(nc, x, itok, cond_w, gate_w, gate_b, exp_w, exp_b, out, y_dram, table):
    B, C, D = x.shape
    NCOND = cond_w.shape[0]
    E, _, H = exp_w.shape
    TOK = B * C
    PAIR = P // C
    KD = D // P
    NH = H // BANK
    NTILE = TOK // P
    G = 8
    NG = NTILE // G
    TPE = TOK // P
    NT = 2 * TOK // P + E - 1
    COLS = E * TPE
    ACOLS = COLS + TPE + E
    RAW = 4
    SLOTW = KD * H

    x_rows = x.rearrange("b c t -> (b c) t")
    w_rows = exp_w.rearrange("e (k p) h -> (e k p) h", p=P)

    with ExitStack() as both:
        def sb(ctx, name, shape, dt=F32):
            return ctx.enter_context(nc.sbuf_tensor(name, shape, dt))

        def pb(ctx, name, shape, dt=F32):
            return ctx.enter_context(nc.psum_tensor(name, shape, dt))

        def sem(name):
            return both.enter_context(nc.semaphore(name))

        raw = sb(both, "raw", [P, RAW, H])
        ident = sb(both, "ident", [P, P])
        idx_all = sb(both, "idx_all", [P, ACOLS], U32)
        tile_e = sb(both, "tile_e", [1, NT], I32)
        tile_s = sb(both, "tile_s", [1, NT], I32)
        tile_c = sb(both, "tile_c", [1, NT], I32)

        s_raw = [sem(f"s_raw{i}") for i in range(RAW)]
        s_dve = sem("s_dve")
        s_split = sem("s_split")

        s_sp = sem("s_sp")
        s_step = sem("s_step")

        def load_chunk(sp, row, k):
            sp.dma_start(raw[:, k % RAW, :], w_rows[bass.ds(row, P), :]).then_inc(s_raw[k % RAW], 16)

        with ExitStack() as ph:
            xs = sb(ph, "xs", [P, G, D])
            ys = sb(ph, "ys", [P, G, D])
            yT = sb(ph, "yT", [P, 2, KD, P])
            bd = sb(ph, "bd", [P, G, P])
            cw = sb(ph, "cw", [P, NCOND, C])
            cond = sb(ph, "cond", [1, B], I32)
            wg = sb(ph, "wg", [P, KD, E])
            gb = sb(ph, "gb", [P, E])
            zero = sb(ph, "zero", [P, D])
            spare = sb(ph, "spare", [P, COLS], U32)
            before = sb(ph, "before", [P, P], BF16)
            ones = sb(ph, "ones", [P, P], BF16)
            ones_f = sb(ph, "ones_f", [P, P])
            rev_i = sb(ph, "rev_i", [P, E], I32)
            rev = sb(ph, "rev", [P, E])
            it_i = sb(ph, "it_i", [1, NT], I32)
            it_f = sb(ph, "it_f", [1, NT])
            tok8 = sb(ph, "tok8", [P, G], U32)
            L = sb(ph, "L", [P, G, E])
            L2 = sb(ph, "L2", [P, G, E])
            eq = sb(ph, "eq", [P, G, E])
            top = sb(ph, "top", [P, G])
            w12 = sb(ph, "w12", [P, 2, G])
            oh = sb(ph, "oh", [P, 2, G, E])
            mask = sb(ph, "mask", [P, G, E], BF16)
            seen = sb(ph, "seen", [P, G + 1, E], BF16)
            picked = sb(ph, "picked", [P, 2, G, E])
            rank_f = sb(ph, "rank_f", [P, 2, G])
            rank = sb(ph, "rank", [P, 2, G], I32)
            hi_i = sb(ph, "hi_i", [P, 2, G], I32)
            lo_i = sb(ph, "lo_i", [P, 2, G], I32)
            adr_i = sb(ph, "adr_i", [P, 2, G], I32)
            e12 = sb(ph, "e12", [P, 2, G])
            adr = sb(ph, "adr", [P, 2, G], U32)
            cnt_f = sb(ph, "cnt_f", [1, E])
            cnt_i = sb(ph, "cnt_i", [1, E], I32)
            ntile_i = sb(ph, "ntile_i", [1, E], I32)
            ntile = sb(ph, "ntile", [1, E])
            base = sb(ph, "base", [1, E])
            jump = sb(ph, "jump", [1, E])
            ge = sb(ph, "ge", [1, NT, E - 1])
            gej = sb(ph, "gej", [1, NT, E - 1])
            sums = sb(ph, "sums", [1, 2, NT])

            psY = [pb(ph, f"psY{i}", [P, D]) for i in range(2)]
            psT = pb(ph, "psT", [P, KD, P])
            psG = pb(ph, "psG", [P, BANK])
            psR = pb(ph, "psR", [P, BANK])

            s_xin = [sem(f"s_xin{i}") for i in range(G)]
            s_xout = [sem(f"s_xout{i}") for i in range(G)]
            s_yout = [sem(f"s_yout{i}") for i in range(G)]
            s_par = sem("s_par")
            s_spare = sem("s_spare")
            s_cond = sem("s_cond")
            s_const = sem("s_const")
            s_clr = sem("s_clr")
            s_bd = sem("s_bd")
            s_y = sem("s_y")
            s_yc = sem("s_yc")
            s_t = sem("s_t")
            s_tc = sem("s_tc")
            s_g = sem("s_g")
            s_L = sem("s_L")
            s_mask = sem("s_mask")
            s_rank = sem("s_rank")
            s_adr = sem("s_adr")
            s_sc = sem("s_sc")
            s_scd = sem("s_scd")
            s_tok = sem("s_tok")
            s_cnt = sem("s_cnt")
            s_tab = sem("s_tab")

            with nc.Block() as block:

                @block.sync
                def _(sp):
                    sp.dma_start(cond[:, :], itok).then_inc(s_cond, 16)
                    for i in range(PAIR):
                        sp.dma_start(cw[C * i:C * (i + 1), :, :],
                                     cond_w.rearrange("n c d -> c n d")).then_inc(s_par, 16)

                    def load(row, s):
                        sp.dma_start(xs[:, s, :], x_rows[bass.ds(row, P), :]).then_inc(s_xin[s], 16)

                    for s in range(G):
                        load(s * P, s)
                        if s == 0:
                            sp.dma_start(wg[:, :, :], gate_w.rearrange("(k p) e -> p k e", p=P)).then_inc(s_par, 16)
                            sp.dma_start(gb[:, :], gate_b.partition_broadcast(P)).then_inc(s_par, 16)

                    def turn(g, more):
                        for s in range(G + G // 2):
                            if s < G:
                                sp.wait_ge(s_xin[s], g * 16 + 16)
                                sp.dma_start(out[bass.ds((g * G + s) * P, P), :], xs[:, s, :]).then_inc(s_xout[s], 16)
                            r = s - G // 2
                            if more and r >= 0:
                                sp.wait_ge(s_y, (g * G + r + 1) + G)
                                sp.wait_ge(s_xout[r], g * 16 + 16)
                                sp.sem_inc(s_sp, 1)
                                load(((g + 1) * G + r) * P, r)

                    with sp.Fori(0, NG - 1, 1) as g:
                        turn(g, True)
                    turn(NG - 1, False)
                    for k in range(RAW):
                        load_chunk(sp, k * P, k)
                    for s in range(G):
                        sp.wait_ge(s_xout[s], 16 * NG)

                @block.gpsimd
                def _(pool):
                    own = Chain(pool, s_clr)
                    own(nc.gpsimd.memset(bd[:, :, :], 0.0))
                    own(nc.gpsimd.memset(ident[:, :], 0.0))
                    nc.gpsimd.memset(ones[:, :], 1.0)
                    own(nc.gpsimd.memset(ones_f[:, :], 1.0))
                    nc.gpsimd.iota(tok8[:, :], pattern=[[P, G]], base=0, channel_multiplier=1)
                    nc.gpsimd.affine_select(out=ident[:, :], in_=ident[:, :], compare_op=ALU.not_equal, fill=1.0,
                                            base=0, pattern=[[-1, P]], channel_multiplier=1)
                    own(nc.gpsimd.affine_select(out=before[:, :], in_=ones_f[:, :], compare_op=ALU.is_gt, fill=0.0,
                                                base=0, pattern=[[1, P]], channel_multiplier=-1))
                    nc.gpsimd.iota(rev_i[:, :], pattern=[[-1, E]], base=E, channel_multiplier=0)
                    nc.gpsimd.iota(it_i[:, :], pattern=[[1, NT]], base=0, channel_multiplier=0)
                    nc.gpsimd.iota(spare[:, :], pattern=[[0, COLS]], base=TOK, channel_multiplier=1)
                    nc.gpsimd.iota(idx_all[:, :], pattern=[[0, ACOLS]], base=TOK, channel_multiplier=1)
                    own(nc.gpsimd.memset(zero[:, :], 0.0))
                    pool.sem_inc(s_const, 1)
                    pool.sem_inc(s_scd, 1)
                    pool.dma_start(table.rearrange("(p c) o -> p (c o)", p=P), spare[:, :]).then_inc(s_spare, 16)
                    pool.dma_start(y_dram[TOK:TOK + P, :], zero[:, :]).then_inc(s_spare, 16)
                    pool.dma_start(out[TOK:TOK + P, :], zero[:, :]).then_inc(s_spare, 16)
                    pool.wait_ge(s_cond, 16)
                    pool.wait_ge(s_par, 16 * (PAIR + 2))

                    def diagonals(g, first=False):
                        for s in range(G):
                            if not first:
                                pool.wait_ge(s_y, g * G + s + 1)
                            for i in range(PAIR):
                                c = pool.value_load(cond[0:1, bass.ds((g * G + s) * PAIR + i, 1)],
                                                    min_val=0, max_val=NCOND - 1)
                                rows = slice(C * i, C * (i + 1))
                                last = nc.gpsimd.tensor_copy(bd[rows, s, C * i:C * (i + 1)],
                                                             cw[rows, bass.ds(c, 1), :].rearrange("p o c -> p (o c)"))
                                last.then_inc(s_bd, 1)
                        pool.wait_ge(s_bd, (g + 1) * (G * PAIR))

                    def scatters(g):
                        pool.wait_ge(s_adr, g + 1)
                        pool.sem_inc(s_step, 1)
                        for r in range(2):
                            for s in range(G):
                                pool.indirect_dma_start(
                                    out=table, out_offset=bass.IndirectOffsetOnAxis(ap=adr[:, r, s:s + 1], axis=0),
                                    in_=tok8[:, s:s + 1], in_offset=None).then_inc(s_sc, 16)
                        pool.wait_ge(s_sc, g * (16 * 2 * G) + 16 * 2 * G)
                        pool.sem_inc(s_scd, 1)
                        nc.gpsimd.tensor_scalar(tok8[:, :], tok8[:, :], G * P, None, ALU.add).then_inc(s_tok, 1)
                        pool.wait_ge(s_tok, g + 1)

                    diagonals(0, first=True)
                    pool.wait_ge(s_spare, 48)
                    with pool.Fori(0, NG - 1, 1) as g:
                        diagonals(g + 1)
                        scatters(g)
                    scatters(NG - 1)
                    pool.dma_start(idx_all[:, 0:COLS], table.rearrange("(p c) o -> p (c o)", p=P)).then_inc(s_tab, 16)
                    pool.wait_ge(s_tab, 16)

                @block.tensor
                def _(pe):
                    pe.sem_inc(s_y, G)
                    pe.sem_inc(s_g, 2)
                    pe.wait_ge(s_const, 1)
                    pe.wait_ge(s_par, 16 * (PAIR + 2))

                    def product(g, s):
                        n = g * G + s
                        pe.wait_ge(s_xin[s], g * 16 + 16)
                        pe.wait_ge(s_bd, (n + 1) * PAIR)
                        pe.wait_ge(s_yc, n + 1)
                        for h in range(D // BANK):
                            last = nc.tensor.matmul(psY[s % 2][:, h * BANK:(h + 1) * BANK], bd[:, s, :],
                                                    xs[:, s, h * BANK:(h + 1) * BANK], start=True, stop=True)
                        last.then_inc(s_y, 1)

                    def transposes(g, s):
                        n = g * G + s
                        pe.wait_ge(s_yc, n + 3)
                        pe.wait_ge(s_tc, n + 1)
                        for k in range(KD):
                            last = nc.tensor.transpose(psT[:, k, :], ys[:, s, k * P:(k + 1) * P], ident[:, :])
                        last.then_inc(s_t, 1)

                    def gate(g, s):
                        n = g * G + s
                        if s == 0:
                            pe.wait_ge(s_L, g + 1)
                        pe.wait_ge(s_tc, n + 2)
                        for k in range(KD):
                            last = nc.tensor.matmul(psG[:, s * E:(s + 1) * E], yT[:, s % 2, k, :], wg[:, k, :],
                                                    start=(k == 0), stop=(k == KD - 1))
                        last.then_inc(s_g, 1)

                    with pe.Fori(0, NG, 1) as g:
                        for s in range(G + 2):
                            if s < G:
                                product(g, s)
                            if 1 <= s <= G:
                                transposes(g, s - 1)
                            if s >= 2:
                                gate(g, s - 2)
                        pe.wait_ge(s_mask, g + 1)
                        nc.tensor.matmul(psR[:, 0:G * E], before[:, :], mask[:, :, :].rearrange("p g e -> p (g e)"),
                                         start=True, stop=False)
                        nc.tensor.matmul(psR[:, 0:G * E], ones[:, :],
                                         seen[:, 0:G, :].rearrange("p g e -> p (g e)"),
                                         start=False, stop=True).then_inc(s_rank, 1)
                    nc.tensor.matmul(psG[:, 0:E], ones[:, :], seen[:, G, :], start=True, stop=True).then_inc(s_cnt, 1)

                @block.scalar
                def _(act):
                    act.sem_inc(s_yc, 2)

                    def turn(g, first=False):
                        for s in range(G):
                            n = g * G + s
                            act.wait_ge(s_y, n + 1 + G)
                            if not first:
                                act.wait_ge(s_yout[s], g * 16)
                            nc.scalar.copy(ys[:, s, :], psY[s % 2][:, :]).then_inc(s_yc, 1)
                            act.wait_ge(s_yc, n + 3)
                            act.dma_start(y_dram[bass.ds(n * P, P), :], ys[:, s, :]).then_inc(s_yout[s], 16)

                    turn(0, first=True)
                    with act.Fori(1, NG, 1) as g:
                        turn(g)
                    for s in range(G):
                        act.wait_ge(s_yout[s], 16 * NG)

                @block.vector
                def _(dve):
                    own = Chain(dve, s_dve)
                    V = nc.vector
                    dve.sem_inc(s_tc, 1)
                    dve.sem_inc(s_L, 1)
                    dve.wait_ge(s_const, 1)
                    V.tensor_copy(it_f[:, :], it_i[:, :])
                    V.tensor_copy(rev[:, :], rev_i[:, :])
                    own(V.memset(seen[:, :, :], 0.0))
                    dve.wait_ge(s_par, 16 * (PAIR + 2))

                    def bc(ap, shape):
                        return ap.to_broadcast(shape)

                    STEPS = 32
                    start = own.n
                    GE = [P, G, E]
                    with dve.Fori(0, NG, 1) as g:
                        own.turn(g * STEPS + start)
                        for s in range(G):
                            n = g * G + s
                            dve.wait_ge(s_t, n + 1)
                            dve.wait_ge(s_g, n + 1)
                            V.tensor_copy(yT[:, s % 2, :, :], psT[:, :, :]).then_inc(s_tc, 1)
                        dve.wait_ge(s_g, g * G + G + 2)
                        V.tensor_tensor(L[:, :, :], psG[:, 0:G * E].rearrange("p (g e) -> p g e", e=E),
                                        gb[:, :].unsqueeze(1).to_broadcast(GE), ALU.add).then_inc(s_L, 1)
                        dve.wait_ge(s_L, g + 2)
                        revb = rev[:, :].unsqueeze(1).to_broadcast(GE)
                        src = L
                        for r in range(2):
                            own(V.tensor_reduce(top[:, :], src[:, :, :], AX.X, ALU.max))
                            own(V.tensor_tensor(eq[:, :, :], src[:, :, :],
                                                top[:, :].unsqueeze(2).to_broadcast(GE), ALU.is_ge))
                            own(V.tensor_tensor(eq[:, :, :], eq[:, :, :], revb, ALU.mult))
                            own(V.tensor_reduce(w12[:, r, :], eq[:, :, :], AX.X, ALU.max))
                            own(V.tensor_tensor(oh[:, r, :, :], w12[:, r, :].unsqueeze(2).to_broadcast(GE), revb,
                                                ALU.is_equal))
                            if r == 0:
                                own(V.scalar_tensor_tensor(L2[:, :, :], oh[:, 0, :, :], -3.0e38, L[:, :, :],
                                                           ALU.mult, ALU.add))
                                src = L2
                        own(V.tensor_tensor(mask[:, :, :], oh[:, 0, :, :], oh[:, 1, :, :], ALU.add))
                        own(V.tensor_copy(seen[:, 0, :], seen[:, G, :]))
                        for s in range(G):
                            own(V.tensor_tensor(seen[:, s + 1, :], seen[:, s, :], mask[:, s, :], ALU.add))
                        dve.sem_inc(s_mask, 1)
                        dve.wait_ge(s_rank, g + 1)
                        own(V.tensor_tensor(picked[:, :, :, :], oh[:, :, :, :],
                                            psR[:, 0:G * E].rearrange("p (g e) -> p g e", e=E).unsqueeze(1)
                                            .to_broadcast([P, 2, G, E]), ALU.mult))
                        own(V.tensor_reduce(rank_f[:, :, :], picked[:, :, :, :], AX.X, ALU.add))
                        own(V.tensor_copy(rank[:, :, :], rank_f[:, :, :]))
                        own(V.tensor_scalar(hi_i[:, :, :], rank[:, :, :], 7, None, ALU.logical_shift_right))
                        own(V.tensor_scalar(lo_i[:, :, :], rank[:, :, :], P - 1, None, ALU.bitwise_and))
                        own(V.tensor_scalar(e12[:, :, :], w12[:, :, :], -TPE, E * TPE, ALU.mult, ALU.add))
                        own(V.tensor_tensor(e12[:, :, :], e12[:, :, :], hi_i[:, :, :], ALU.add))
                        dve.wait_ge(s_scd, g + 1)
                        own(V.scalar_tensor_tensor(adr[:, :, :], lo_i[:, :, :], COLS, e12[:, :, :],
                                                   ALU.mult, ALU.add))
                        dve.sem_inc(s_adr, 1)
                        assert own.n <= STEPS, own.n
                        if own.n < STEPS:
                            dve.sem_inc(s_dve, STEPS - own.n)
                    own.turn(NG * STEPS + start)
                    dve.wait_ge(s_cnt, 1)
                    own(V.tensor_scalar(cnt_f[:, :], psG[0:1, 0:E], P - 1, None, ALU.add))
                    own(V.tensor_copy(cnt_i[:, :], cnt_f[:, :]))
                    own(V.tensor_scalar(ntile_i[:, :], cnt_i[:, :], 7, None, ALU.logical_shift_right))
                    V.tensor_copy(ntile[:, :], ntile_i[:, :])
                    own(V.memset(base[:, :], 0.0))
                    for e in range(1, E):
                        own(V.tensor_tensor(base[:, e:e + 1], base[:, e - 1:e], ntile[:, e - 1:e], ALU.add))
                    own(V.tensor_scalar(jump[:, :], ntile[:, :], -1.0, TPE, ALU.mult, ALU.add))
                    SH = [1, NT, E - 1]
                    own(V.tensor_tensor(ge[:, :, :], it_f[:, :].unsqueeze(2).to_broadcast(SH),
                                        base[:, 1:E].unsqueeze(1).to_broadcast(SH), ALU.is_ge))
                    own(V.tensor_tensor(gej[:, :, :], ge[:, :, :], jump[:, 0:E - 1].unsqueeze(1).to_broadcast(SH),
                                        ALU.mult))
                    own(V.tensor_reduce(sums[:, 0, :], ge[:, :, :], AX.X, ALU.add))
                    own(V.tensor_reduce(sums[:, 1, :], gej[:, :, :], AX.X, ALU.add))
                    own(V.tensor_copy(tile_e[:, :], sums[:, 0, :]))
                    own(V.tensor_tensor(tile_c[:, :], sums[:, 1, :], it_f[:, :], ALU.add))
                    own(V.tensor_scalar(tile_s[:, :], sums[:, 0, :], 2.0, E, ALU.add, ALU.min))

        with ExitStack() as ph:
            w_hi = sb(ph, "w_hi", [P, 2 * SLOTW], F32R)
            w_lo = sb(ph, "w_lo", [P, 2 * SLOTW], F32R)
            bias = sb(ph, "bias", [P, 2 * H])
            NY = 2
            yg = sb(ph, "yg", [P, NY, D])
            a_hi = sb(ph, "a_hi", [P, 2, D], F32R)
            a_lo = sb(ph, "a_lo", [P, 2, D], F32R)
            o_sb = sb(ph, "o_sb", [P, 2, H])
            idx_g = sb(ph, "idx_g", [P, 2], U32)
            idx_s = sb(ph, "idx_s", [P, 2], U32)
            psT = [pb(ph, f"psT2{i}", [P, D]) for i in range(2)]
            psO = [pb(ph, f"psO{i}", [P, H]) for i in range(2)]

            s_bias = sem("s_bias")
            s_hi = sem("s_hi")
            s_yg = [sem(f"s_yg{i}") for i in range(2)]
            s_ix = sem("s_ix")
            s_tr = sem("s_tr")
            s_ahi = sem("s_ahi")
            s_alo = sem("s_alo")
            s_mm = sem("s_mm")
            s_bo = sem("s_bo")
            s_out = sem("s_out")
            s_add = sem("s_add")

            with nc.Block() as block:

                @block.sync
                def _(sp):
                    def expert(e, first):
                        for k in range(first, KD):
                            sp.wait_ge(s_split, e * KD + k - RAW + 1)
                            sp.sem_inc(s_sp, 1)
                            load_chunk(sp, e * D + k * P, k)
                        sp.wait_ge(s_split, e * KD + 1)
                        sp.sem_inc(s_sp, 1)
                        sp.dma_start(bias[:, bass.ds((e % 2) * H, H)],
                                     exp_b[bass.ds(e, 1), :].rearrange("o h -> (o h)").partition_broadcast(P)
                                     ).then_inc(s_bias, 16)
                    expert(0, RAW)
                    with sp.Fori(1, E, 1) as e:
                        expert(e, 0)

                @block.gpsimd
                def _(pool):
                    cnt = [0]

                    def gather(t, slot, count):
                        c = pool.value_load(tile_c[0:1, bass.ds(t, 1)], min_val=0, max_val=ACOLS - 1)
                        nc.gpsimd.tensor_copy(idx_g[:, slot:slot + 1], idx_all[:, bass.ds(c, 1)]).then_inc(s_ix, 1)
                        pool.wait_ge(s_ix, count + 1)
                        pool.sem_inc(s_step, 1)
                        pool.indirect_dma_start(
                            out=yg[:, slot, :], out_offset=None, in_=y_dram,
                            in_offset=bass.IndirectOffsetOnAxis(ap=idx_g[:, slot:slot + 1], axis=0)
                        ).then_inc(s_yg[slot], 16)

                    def scatter(t, slot, count, first=False):
                        if not first:
                            pool.wait_ge(s_add, t * 16)
                        c = pool.value_load(tile_c[0:1, bass.ds(t, 1)], min_val=0, max_val=ACOLS - 1)
                        nc.gpsimd.tensor_copy(idx_s[:, slot:slot + 1], idx_all[:, bass.ds(c, 1)]).then_inc(s_ix, 1)
                        pool.wait_ge(s_ix, count + 1)
                        pool.wait_ge(s_out, t + 1)
                        pool.sem_inc(s_step, 1)
                        pool.indirect_dma_start(
                            out=out, out_offset=bass.IndirectOffsetOnAxis(ap=idx_s[:, slot:slot + 1], axis=0),
                            in_=o_sb[:, slot, :], in_offset=None, compute_op=ALU.add).then_inc(s_add, 16)

                    gather(0, 0, 0)
                    gather(1, 1, 1)
                    pool.wait_ge(s_tr, 1)
                    gather(2, 0, 2)
                    scatter(0, 0, 3, first=True)
                    with pool.Fori(0, (NT - 3) // 2, 1) as i:
                        for j in range(2):
                            t = i * 2 + (j + 1)
                            pool.wait_ge(s_tr, t + 1)
                            gather(t + 2, (j + 1) % 2, i * 4 + (2 * j + 4))
                            scatter(t, (j + 1) % 2, i * 4 + (2 * j + 5))
                    for t in range(NT - 2, NT):
                        scatter(t, t % 2, 2 * (NT - 3) + 4 + t - (NT - 2))
                    pool.wait_ge(s_add, 16 * NT)

                def split_to(eng, reg, target, body):
                    with eng.While(lambda: eng.snap(reg) < target):
                        body(eng.snap(reg))
                        eng.reg_add(reg, reg, 1)

                def tiles(eng, parts, finish, ahead, reg, split):
                    parts(0, 0)
                    first = eng.value_load(tile_e[0:1, 0:1], min_val=0, max_val=E - 1)
                    split_to(eng, reg, eng.snap(first + 1), split)
                    ahead(0)
                    for v in (1, 2):
                        parts(v, v % 2)
                        finish(v - 1, (v - 1) % 2, True)
                        ahead(v)
                    with eng.Fori(0, (NT - 3) // 2, 1) as i:
                        for j in range(2):
                            v = i * 2 + (3 + j)
                            parts(v, (1 + j) % 2)
                            finish(i * 2 + (2 + j), j, False)
                            ahead(v)
                    finish(NT - 1, (NT - 1) % 2, False)

                @block.tensor
                def _(pe):
                    pe.sem_inc(s_mm, 2)

                    def transposes(t, s):
                        pe.wait_ge(s_yg[s], (t // 2) * 16 + 16)
                        pe.wait_ge(s_alo, t + 1)
                        for k in range(KD):
                            last = nc.tensor.transpose(psT[s][:, k * P:(k + 1) * P], yg[:, s, k * P:(k + 1) * P],
                                                       ident[:, :])
                        last.then_inc(s_tr, 1)

                    def products(t, s):
                        e = pe.value_load(tile_e[0:1, bass.ds(t, 1)], min_val=0, max_val=E - 1)
                        slot = pe.snap((e % 2) * SLOTW)
                        pe.wait_ge(s_alo, t + 3)
                        pe.wait_ge(s_split, (e + 1) * KD)
                        pe.wait_ge(s_bo, t + 1)
                        for k in range(KD):
                            for a, ws in ((a_hi, (w_hi, w_lo)), (a_lo, (w_hi,))):
                                for w in ws:
                                    for h in range(NH):
                                        last = nc.tensor.matmul(
                                            psO[s][:, h * BANK:(h + 1) * BANK], a[:, s, k * P:(k + 1) * P],
                                            w[:, bass.ds(slot + (k * H + h * BANK), BANK)],
                                            start=(k == 0 and a is a_hi and w is w_hi),
                                            stop=(k == KD - 1 and a is a_lo))
                        last.then_inc(s_mm, 1)

                    transposes(0, 0)
                    with pe.Fori(0, (NT - 1) // 2, 1) as i:
                        for j in range(2):
                            t = i * 2 + j
                            transposes(t + 1, (j + 1) % 2)
                            products(t, j)
                    products(NT - 1, 0)

                @block.scalar
                def _(act):
                    reg = act.alloc_register("split_a")
                    act.reg_mov(reg, 0)

                    def split(x):
                        slot = act.snap((x % 2) * SLOTW)
                        for k in range(KD):
                            act.wait_ge(s_raw[k % RAW], x * (16 * KD // RAW) + 16 * (k // RAW + 1))
                            nc.scalar.copy(w_hi[:, bass.ds(slot + k * H, H)], raw[:, k % RAW, :]).then_inc(s_hi, 1)

                    def parts(t, s):
                        act.wait_ge(s_tr, t + 1)
                        act.wait_ge(s_mm, t + 1)
                        nc.scalar.copy(a_hi[:, s, :], psT[s][:, :]).then_inc(s_ahi, 1)

                    def finish(t, s, first):
                        act.wait_ge(s_bo, t + 3)
                        nc.scalar.activation(o_sb[:, s, :], o_sb[:, s, :], ACTF.Relu, scale=0.5).then_inc(s_out, 1)

                    def ahead(t):
                        split_to(act, reg, act.value_load(tile_s[0:1, bass.ds(t, 1)], min_val=0, max_val=E), split)

                    tiles(act, parts, finish, ahead, reg, split)

                @block.vector
                def _(dve):
                    reg = dve.alloc_register("split_v")
                    dve.reg_mov(reg, 0)
                    dve.sem_inc(s_alo, 2)
                    dve.sem_inc(s_bo, 2)

                    def split(x):
                        slot = dve.snap((x % 2) * SLOTW)
                        for k in range(KD):
                            dve.wait_ge(s_raw[k % RAW], x * (16 * KD // RAW) + 16 * (k // RAW + 1))
                            dve.wait_ge(s_hi, x * KD + k + 1)
                            nc.vector.tensor_tensor(w_lo[:, bass.ds(slot + k * H, H)], raw[:, k % RAW, :],
                                                    w_hi[:, bass.ds(slot + k * H, H)],
                                                    ALU.subtract).then_inc(s_split, 1)
                        dve.wait_ge(s_bias, x * 16 + 16)

                    def parts(t, s):
                        dve.wait_ge(s_ahi, t + 1)
                        dve.wait_ge(s_mm, t + 1)
                        nc.vector.tensor_tensor(a_lo[:, s, :], psT[s][:, :], a_hi[:, s, :],
                                                ALU.subtract).then_inc(s_alo, 1)

                    def finish(t, s, first):
                        e = dve.value_load(tile_e[0:1, bass.ds(t, 1)], min_val=0, max_val=E - 1)
                        dve.wait_ge(s_mm, t + 3)
                        if not first:
                            dve.wait_ge(s_add, (t - 1) * 16)
                        nc.vector.tensor_tensor(o_sb[:, s, :], psO[s][:, :], bias[:, bass.ds((e % 2) * H, H)],
                                                ALU.add).then_inc(s_bo, 1)

                    def ahead(t):
                        split_to(dve, reg, dve.value_load(tile_s[0:1, bass.ds(t, 1)], min_val=0, max_val=E), split)

                    tiles(dve, parts, finish, ahead, reg, split)


_INS = ["x", "itok_B_0_15", "L0_cond_weights", "L0_ffn_W_gate", "L0_ffn_b_gate", "L0_ffn_W_e", "L0_ffn_b_e"]


def kernel(**inputs):
    import numpy as _np
    import concourse.bacc as _bacc
    from concourse import mybir as _mybir
    from concourse.bass_utils import run_bass_kernel_spmd as _run

    nc = _bacc.Bacc("TRN2", target_bir_lowering=False, num_devices=1)
    arrays, aps = {}, []
    for name in _INS:
        a = _np.ascontiguousarray(inputs[name])
        if name == "itok_B_0_15":
            a = a.reshape(1, -1)
        arrays[f"in_{name}"] = a
        aps.append(nc.dram_tensor(f"in_{name}", a.shape, _mybir.dt.from_np(a.dtype), kind="ExternalInput").ap())
    batches, channels, features = arrays["in_x"].shape
    experts = arrays["in_L0_ffn_W_e"].shape[0]
    tokens = batches * channels
    out = nc.dram_tensor("out", (tokens + P, features), F32, kind="ExternalOutput").ap()
    y_dram = nc.dram_tensor("y_rows", (tokens + P, features), F32).ap()
    table = nc.dram_tensor("slot_table", (experts * tokens, 1), U32).ap()
    build(nc, *aps, out, y_dram, table)
    r = _run(nc, [arrays], core_ids=[0])
    return r.results[0]["out"][:tokens].reshape(batches, channels, features)
```

```python
from contextlib import ExitStack

import numpy as np
import concourse.bass as bass
from concourse import mybir
from concourse.alu_op_type import AluOpType as ALU

P = 128
F32, F32R, BF16 = mybir.dt.float32, mybir.dt.float32r, mybir.dt.bfloat16
I32, U32 = mybir.dt.int32, mybir.dt.uint32
ACTF = mybir.ActivationFunctionType
AX = mybir.AxisListType
BANK = 512


class Chain:

    def __init__(self, eng, sem):
        self.eng, self.sem, self.base, self.n = eng, sem, 0, 0

    def turn(self, base):
        self.base, self.n = base, 0

    def __call__(self, ins):
        self.n += 1
        ins.then_inc(self.sem, 1)
        self.eng.wait_ge(self.sem, self.base + self.n)


def build(nc, x, itok, cond_w, gate_w, gate_b, exp_w, exp_b, out, y_dram, table):
    B, C, D = x.shape
    NCOND = cond_w.shape[0]
    E, _, H = exp_w.shape
    TOK = B * C
    PAIR = P // C
    KD = D // P
    NH = H // BANK
    NTILE = TOK // P
    G = 4
    NG = NTILE // G
    TPE = TOK // P
    NT = 2 * TOK // P + E - 1
    NL = NT + 2
    COLS = E * TPE
    ACOLS = COLS + TPE + E
    RAW = 4
    HALF = RAW * H
    SURE = 2 * TOK // P

    x_rows = x.rearrange("b c t -> (b c) t")
    w_rows = exp_w.rearrange("e (k p) h -> (e k p) h", p=P)

    with ExitStack() as both:
        def sb(ctx, name, shape, dt=F32):
            return ctx.enter_context(nc.sbuf_tensor(name, shape, dt))

        def pb(ctx, name, shape, dt=F32):
            return ctx.enter_context(nc.psum_tensor(name, shape, dt))

        def sem(name):
            return both.enter_context(nc.semaphore(name))

        w_hi = sb(both, "w_hi", [P, 4 * HALF], F32R)
        w_lo = sb(both, "w_lo", [P, 4 * HALF], F32R)
        raw = sb(both, "raw", [P, RAW, H])
        ident = sb(both, "ident", [P, P])
        idx_all = sb(both, "idx_all", [P, ACOLS], U32)
        tile_e = sb(both, "tile_e", [1, NL], I32)
        tile_s = sb(both, "tile_s", [1, NL], I32)
        tiles_n = sb(both, "tiles_n", [1, 1], I32)
        tile_c = sb(both, "tile_c", [1, NL], I32)

        s_raw = [sem(f"s_raw{i}") for i in range(RAW)]
        s_dve = sem("s_dve")
        s_hi = sem("s_hi")
        s_split = sem("s_split")

        s_sp = sem("s_sp")
        s_step = sem("s_step")

        def load_chunk(sp, row, k):
            sp.dma_start(raw[:, k % RAW, :], w_rows[bass.ds(row, P), :]).then_inc(s_raw[k % RAW], 16)

        def split_hi(act, h):
            for k in range(RAW):
                at = (h % 4) * HALF + k * H
                act.wait_ge(s_raw[k], h * 16 + 16)
                nc.scalar.copy(w_hi[:, bass.ds(at, H)], raw[:, k, :]).then_inc(s_hi, 1)

        def split_lo(dve, h):
            for k in range(RAW):
                at = (h % 4) * HALF + k * H
                dve.wait_ge(s_raw[k], h * 16 + 16)
                dve.wait_ge(s_hi, h * RAW + (k + 1))
                nc.vector.tensor_tensor(w_lo[:, bass.ds(at, H)], raw[:, k, :], w_hi[:, bass.ds(at, H)],
                                        ALU.subtract).then_inc(s_split, 1)

        with ExitStack() as ph:
            xs = sb(ph, "xs", [P, G, D])
            ys = sb(ph, "ys", [P, G, D])
            yT = sb(ph, "yT", [P, 2, KD, P])
            bd = sb(ph, "bd", [P, G, P])
            cw = sb(ph, "cw", [P, NCOND, C])
            cond = sb(ph, "cond", [1, B], I32)
            wg = sb(ph, "wg", [P, KD, E])
            gb = sb(ph, "gb", [P, E])
            zero = sb(ph, "zero", [P, D])
            warm = sb(ph, "warm", [1, 2])
            spare = sb(ph, "spare", [P, COLS], U32)
            before = sb(ph, "before", [P, P], BF16)
            ones = sb(ph, "ones", [P, P], BF16)
            ones_f = sb(ph, "ones_f", [P, P])
            rev_i = sb(ph, "rev_i", [P, E], I32)
            rev = sb(ph, "rev", [P, E])
            it_i = sb(ph, "it_i", [1, NL], I32)
            it_f = sb(ph, "it_f", [1, NL])
            toks = sb(ph, "toks", [P, 2, G], U32)
            L = sb(ph, "L", [P, G, E])
            L2 = sb(ph, "L2", [P, G, E])
            eq = sb(ph, "eq", [P, G, E])
            top = sb(ph, "top", [P, G])
            w12 = sb(ph, "w12", [P, 2, G])
            oh = sb(ph, "oh", [P, 2, G, E])
            mask = sb(ph, "mask", [P, G, E], BF16)
            seen = sb(ph, "seen", [P, G + 1, E], BF16)
            picked = sb(ph, "picked", [P, 2, G, E])
            rank_f = sb(ph, "rank_f", [P, 2, G])
            rank = sb(ph, "rank", [P, 2, G], I32)
            rank_tile = sb(ph, "rank_tile", [P, 2, G], I32)
            rank_row = sb(ph, "rank_row", [P, 2, G], I32)
            col = sb(ph, "col", [P, 2, G])
            adr = sb(ph, "adr", [P, 2, 2, G], U32)
            cnt_f = sb(ph, "cnt_f", [1, E])
            cnt_i = sb(ph, "cnt_i", [1, E], I32)
            ntile_i = sb(ph, "ntile_i", [1, E], I32)
            ntile = sb(ph, "ntile", [1, E])
            base = sb(ph, "base", [1, E + 1])
            jump = sb(ph, "jump", [1, E])
            ge = sb(ph, "ge", [1, NL, E - 1])
            gej = sb(ph, "gej", [1, NL, E - 1])
            sums = sb(ph, "sums", [1, 2, NL])
            halves = sb(ph, "halves", [1, NL])

            psY = [pb(ph, f"psY{i}", [P, D]) for i in range(2)]
            psT = pb(ph, "psT", [P, KD, P])
            psG = pb(ph, "psG", [P, BANK])
            psR = pb(ph, "psR", [P, BANK])

            s_xin = [sem(f"s_xin{i}") for i in range(G)]
            s_xout = [sem(f"s_xout{i}") for i in range(G)]
            s_yout = [sem(f"s_yout{i}") for i in range(G)]
            s_cw = sem("s_cw")
            s_gw = sem("s_gw")
            s_spare = sem("s_spare")
            s_const = sem("s_const")
            s_clr = sem("s_clr")
            s_bd0 = sem("s_bd0")
            s_bd = sem("s_bd")
            s_y = sem("s_y")
            s_yc = sem("s_yc")
            s_t = sem("s_t")
            s_tc = sem("s_tc")
            s_g = sem("s_g")
            s_L = sem("s_L")
            s_mask = sem("s_mask")
            s_rank = sem("s_rank")
            s_adr = sem("s_adr")
            s_sc = [sem(f"s_sc{i}") for i in range(2)]
            s_scd = sem("s_scd")
            s_tok = sem("s_tok")
            s_cnt = sem("s_cnt")
            s_tab = sem("s_tab")

            with nc.Block() as block:

                @block.sync
                def _(sp):
                    def load(row, s):
                        sp.dma_start(xs[:, s, :], x_rows[bass.ds(row, P), :]).then_inc(s_xin[s], 16)

                    sp.dma_start(cond[:, :], itok).then_inc(s_cw, 16)
                    for i in range(PAIR):
                        sp.dma_start(cw[C * i:C * (i + 1), :, :],
                                     cond_w.rearrange("n c d -> c n d")).then_inc(s_cw, 16)
                    for s in range(G):
                        load(s * P, s)
                        if s == 0:
                            sp.dma_start(wg[:, :, :], gate_w.rearrange("(k p) e -> p k e", p=P)).then_inc(s_gw, 16)
                            sp.dma_start(gb[:, :], gate_b.partition_broadcast(P)).then_inc(s_gw, 16)

                    def turn(g, more):
                        for s in range(G + 2):
                            if s < G:
                                sp.wait_ge(s_xin[s], g * 16 + 16)
                                sp.dma_start(out[bass.ds((g * G + s) * P, P), :], xs[:, s, :]).then_inc(s_xout[s], 16)
                            r = s - 2
                            if more and r >= 0:
                                sp.wait_ge(s_y, (g * G + r + 1) + G)
                                sp.wait_ge(s_xout[r], g * 16 + 16)
                                sp.sem_inc(s_sp, 1)
                                load(((g + 1) * G + r) * P, r)

                    with sp.Fori(0, NG - 1, 1) as g:
                        turn(g, True)
                    turn(NG - 1, False)
                    for k in range(KD):
                        if k >= RAW:
                            sp.wait_ge(s_split, k - RAW + 1)
                        load_chunk(sp, k * P, k)
                    for s in range(G):
                        sp.wait_ge(s_xout[s], 16 * NG)

                @block.gpsimd
                def _(pool):
                    own = Chain(pool, s_clr)
                    own(nc.gpsimd.memset(ident[:, :], 0.0))
                    nc.gpsimd.memset(ones[:, :], 1.0)
                    own(nc.gpsimd.memset(ones_f[:, :], 1.0))
                    nc.gpsimd.affine_select(out=ident[:, :], in_=ident[:, :], compare_op=ALU.not_equal, fill=1.0,
                                            base=0, pattern=[[-1, P]], channel_multiplier=1)
                    own(nc.gpsimd.affine_select(out=before[:, :], in_=ones_f[:, :], compare_op=ALU.is_gt, fill=0.0,
                                                base=0, pattern=[[1, P]], channel_multiplier=-1))
                    nc.gpsimd.iota(rev_i[:, :], pattern=[[-1, E]], base=E, channel_multiplier=0)
                    own(nc.gpsimd.iota(it_i[:, :], pattern=[[1, NL]], base=0, channel_multiplier=0))
                    pool.sem_inc(s_const, 1)
                    nc.gpsimd.iota(toks[:, :, :], pattern=[[G * P, 2], [P, G]], base=0, channel_multiplier=1)
                    nc.gpsimd.iota(spare[:, :], pattern=[[0, COLS]], base=TOK, channel_multiplier=1)
                    nc.gpsimd.iota(idx_all[:, :], pattern=[[0, ACOLS]], base=TOK, channel_multiplier=1)
                    own(nc.gpsimd.memset(zero[:, :], 0.0))
                    pool.sem_inc(s_scd, 2)
                    pool.dma_start(table.rearrange("(p c) o -> p (c o)", p=P), spare[:, :]).then_inc(s_spare, 16)
                    pool.dma_start(y_dram[TOK:TOK + P, :], zero[:, :]).then_inc(s_spare, 16)
                    pool.dma_start(out[TOK:TOK + P, :], zero[:, :]).then_inc(s_spare, 16)
                    pool.wait_ge(s_spare, 48)
                    LAND = 16 * 2 * G

                    def turn(g, p, pairs):
                        pool.wait_ge(s_adr, g + 1)
                        pool.sem_inc(s_step, 1)
                        for r in range(2):
                            for s in range(G):
                                pool.indirect_dma_start(
                                    out=table, out_offset=bass.IndirectOffsetOnAxis(ap=adr[:, p, r, s:s + 1], axis=0),
                                    in_=toks[:, p, s:s + 1], in_offset=None).then_inc(s_sc[p], 16)
                        if pairs is not None:
                            pool.wait_ge(s_sc[1 - p], pairs * LAND)
                            pool.sem_inc(s_scd, 1)
                            nc.gpsimd.tensor_scalar(toks[:, 1 - p, :], toks[:, 1 - p, :], 2 * G * P, None,
                                                    ALU.add).then_inc(s_tok, 1)
                            pool.wait_ge(s_tok, g)

                    turn(0, 0, None)
                    turn(1, 1, 1)
                    with pool.Fori(1, NG // 2, 1) as i:
                        turn(i * 2, 0, i)
                        turn(i * 2 + 1, 1, i + 1)
                    pool.wait_ge(s_sc[1], NG // 2 * LAND)
                    pool.dma_start(idx_all[:, 0:COLS], table.rearrange("(p c) o -> p (c o)", p=P)).then_inc(s_tab, 16)
                    pool.wait_ge(s_tab, 16)

                @block.tensor
                def _(pe):
                    pe.sem_inc(s_y, G)
                    pe.sem_inc(s_g, 2)

                    def product(g, s):
                        n = g * G + s
                        pe.wait_ge(s_xin[s], g * 16 + 16)
                        pe.wait_ge(s_bd, (n + 1) * PAIR)
                        pe.wait_ge(s_yc, n + 1)
                        for h in range(D // BANK):
                            last = nc.tensor.matmul(psY[s % 2][:, h * BANK:(h + 1) * BANK], bd[:, s, :],
                                                    xs[:, s, h * BANK:(h + 1) * BANK], start=True, stop=True)
                        last.then_inc(s_y, 1)

                    def transposes(g, s):
                        n = g * G + s
                        pe.wait_ge(s_yc, n + 3)
                        pe.wait_ge(s_tc, n + 1)
                        for k in range(KD):
                            last = nc.tensor.transpose(psT[:, k, :], ys[:, s, k * P:(k + 1) * P], ident[:, :])
                        last.then_inc(s_t, 1)

                    def gate(g, s):
                        n = g * G + s
                        if s == 0:
                            pe.wait_ge(s_L, g + 1)
                        pe.wait_ge(s_tc, n + 2)
                        for k in range(KD):
                            last = nc.tensor.matmul(psG[:, s * E:(s + 1) * E], yT[:, s % 2, k, :], wg[:, k, :],
                                                    start=(k == 0), stop=(k == KD - 1))
                        last.then_inc(s_g, 1)

                    def ranks(g):
                        pe.wait_ge(s_mask, g + 1)
                        nc.tensor.matmul(psR[:, 0:G * E], before[:, :], mask[:, :, :].rearrange("p g e -> p (g e)"),
                                         start=True, stop=False)
                        nc.tensor.matmul(psR[:, 0:G * E], ones[:, :],
                                         seen[:, 0:G, :].rearrange("p g e -> p (g e)"),
                                         start=False, stop=True).then_inc(s_rank, 1)

                    def turn(g, first=False, last=False):
                        for s in range(G):
                            if s == G - 1 and not first:
                                ranks(g - 1)
                            if not (last and s >= G - 2):
                                product(g + (s + 2) // G, (s + 2) % G)
                            if not (last and s == G - 1):
                                transposes(g + (s + 1) // G, (s + 1) % G)
                            gate(g, s)

                    product(0, 0)
                    product(0, 1)
                    pe.wait_ge(s_const, 1)
                    transposes(0, 0)
                    pe.wait_ge(s_gw, 32)
                    turn(0, first=True)
                    with pe.Fori(1, NG - 1, 1) as g:
                        turn(g)
                    turn(NG - 1, last=True)
                    ranks(NG - 1)
                    nc.tensor.matmul(psG[:, 0:E], ones[:, :], seen[:, G, :], start=True, stop=True).then_inc(s_cnt, 1)

                @block.scalar
                def _(act):
                    act.sem_inc(s_yc, 2)
                    act.wait_ge(s_bd0, 1)
                    nc.scalar.activation(warm[:, :], warm[:, :], ACTF.Relu)
                    act.wait_ge(s_cw, 16 * (PAIR + 1))
                    act.wait_ge(s_bd0, 2)

                    def diagonal(n, s):
                        for i in range(PAIR):
                            c = act.value_load(cond[0:1, bass.ds(n * PAIR + i, 1)], min_val=0, max_val=NCOND - 1)
                            rows = slice(C * i, C * (i + 1))
                            nc.scalar.copy(bd[rows, s, C * i:C * (i + 1)],
                                           cw[rows, bass.ds(c, 1), :].rearrange("p o c -> p (o c)")).then_inc(s_bd, 1)

                    def turn(g, first=False, last=False):
                        for s in range(G):
                            n = g * G + s
                            act.wait_ge(s_y, n + 1 + G)
                            if not first:
                                act.wait_ge(s_yout[s], g * 16)
                            nc.scalar.copy(ys[:, s, :], psY[s % 2][:, :]).then_inc(s_yc, 1)
                            act.wait_ge(s_yc, n + 3)
                            act.dma_start(y_dram[bass.ds(n * P, P), :], ys[:, s, :]).then_inc(s_yout[s], 16)
                            if not last:
                                diagonal(n + G, s)

                    for s in range(G):
                        diagonal(s, s)
                    turn(0, first=True)
                    with act.Fori(1, NG - 1, 1) as g:
                        turn(g)
                    turn(NG - 1, last=True)
                    for h in range(2):
                        split_hi(act, h)
                    for s in range(G):
                        act.wait_ge(s_yout[s], 16 * NG)

                @block.vector
                def _(dve):
                    own = Chain(dve, s_dve)
                    V = nc.vector
                    V.memset(warm[:, :], 0.0).then_inc(s_bd0, 1)
                    V.memset(bd[:, :, :], 0.0).then_inc(s_bd0, 1)
                    dve.sem_inc(s_tc, 1)
                    dve.sem_inc(s_L, 1)
                    own(V.memset(seen[:, :, :], 0.0))
                    dve.wait_ge(s_const, 1)
                    V.tensor_copy(it_f[:, :], it_i[:, :])
                    own(V.tensor_copy(rev[:, :], rev_i[:, :]))
                    dve.wait_ge(s_gw, 32)
                    GE = [P, G, E]
                    revb = rev[:, :].unsqueeze(1).to_broadcast(GE)

                    def copy(n, s):
                        dve.wait_ge(s_t, n + 1)
                        dve.wait_ge(s_g, n + 1)
                        V.tensor_copy(yT[:, s % 2, :, :], psT[:, :, :]).then_inc(s_tc, 1)

                    def logits(g):
                        dve.wait_ge(s_g, g * G + (G + 2))
                        V.tensor_tensor(L[:, :, :], psG[:, 0:G * E].rearrange("p (g e) -> p g e", e=E),
                                        gb[:, :].unsqueeze(1).to_broadcast(GE), ALU.add).then_inc(s_L, 1)

                    def choose(g, r):
                        if r == 0:
                            dve.wait_ge(s_L, g + 2)
                        src = (L, L2)[r]
                        own(V.tensor_reduce(top[:, :], src[:, :, :], AX.X, ALU.max))
                        own(V.tensor_tensor(eq[:, :, :], src[:, :, :],
                                            top[:, :].unsqueeze(2).to_broadcast(GE), ALU.is_ge))
                        own(V.tensor_tensor(eq[:, :, :], eq[:, :, :], revb, ALU.mult))
                        own(V.tensor_reduce(w12[:, r, :], eq[:, :, :], AX.X, ALU.max))
                        own(V.tensor_tensor(oh[:, r, :, :], w12[:, r, :].unsqueeze(2).to_broadcast(GE), revb,
                                            ALU.is_equal))
                        if r == 0:
                            own(V.scalar_tensor_tensor(L2[:, :, :], oh[:, 0, :, :], -3.0e38, L[:, :, :],
                                                       ALU.mult, ALU.add))

                    def masks():
                        own(V.tensor_tensor(mask[:, :, :], oh[:, 0, :, :], oh[:, 1, :, :], ALU.add))
                        own(V.tensor_copy(seen[:, 0, :], seen[:, G, :]))
                        for s in range(G):
                            own(V.tensor_tensor(seen[:, s + 1, :], seen[:, s, :], mask[:, s, :], ALU.add))
                        dve.sem_inc(s_mask, 1)

                    def slots(g):
                        dve.wait_ge(s_rank, g + 1)
                        own(V.tensor_tensor(picked[:, :, :, :], oh[:, :, :, :],
                                            psR[:, 0:G * E].rearrange("p (g e) -> p g e", e=E).unsqueeze(1)
                                            .to_broadcast([P, 2, G, E]), ALU.mult))
                        own(V.tensor_reduce(rank_f[:, :, :], picked[:, :, :, :], AX.X, ALU.add))
                        own(V.tensor_copy(rank[:, :, :], rank_f[:, :, :]))
                        V.tensor_scalar(rank_tile[:, :, :], rank[:, :, :], 7, None, ALU.logical_shift_right)
                        V.tensor_scalar(rank_row[:, :, :], rank[:, :, :], P - 1, None, ALU.bitwise_and)
                        own(V.tensor_scalar(col[:, :, :], w12[:, :, :], -TPE, E * TPE, ALU.mult, ALU.add))
                        own(V.tensor_tensor(col[:, :, :], col[:, :, :], rank_tile[:, :, :], ALU.add))
                        dve.wait_ge(s_scd, g + 1)
                        own(V.scalar_tensor_tensor(adr[:, bass.ds(g % 2, 1), :, :].rearrange("p o r s -> p (o r) s"),
                                                   rank_row[:, :, :], COLS, col[:, :, :],
                                                   ALU.mult, ALU.add))
                        dve.sem_inc(s_adr, 1)

                    start = own.n
                    STEPS = 11 + 2 + G + 6

                    def turn(g, last=False):
                        own.turn((g - 1) * STEPS + start)
                        logits(g - 1)
                        copy(g * G + 1, 1)
                        choose(g - 1, 0)
                        copy(g * G + 2, 2)
                        choose(g - 1, 1)
                        masks()
                        copy(g * G + 3, 3)
                        if not last:
                            copy(g * G + 4, 0)
                        slots(g - 1)
                        assert own.n == STEPS, own.n

                    for s in range(G + 1):
                        copy(s, s)
                    with dve.Fori(1, NG - 1, 1) as g:
                        turn(g)
                    turn(NG - 1, last=True)
                    own.turn((NG - 1) * STEPS + start)
                    logits(NG - 1)
                    choose(NG - 1, 0)
                    choose(NG - 1, 1)
                    masks()
                    slots(NG - 1)
                    dve.wait_ge(s_cnt, 1)
                    own(V.tensor_scalar(cnt_f[:, :], psG[0:1, 0:E], P - 1, None, ALU.add))
                    own(V.tensor_copy(cnt_i[:, :], cnt_f[:, :]))
                    own(V.tensor_scalar(ntile_i[:, :], cnt_i[:, :], 7, None, ALU.logical_shift_right))
                    V.tensor_copy(ntile[:, :], ntile_i[:, :])
                    own(V.memset(base[:, :], 0.0))
                    for e in range(1, E + 1):
                        own(V.tensor_tensor(base[:, e:e + 1], base[:, e - 1:e], ntile[:, e - 1:e], ALU.add))
                    V.tensor_copy(tiles_n[:, :], base[:, E:E + 1])
                    own(V.tensor_scalar(jump[:, :], ntile[:, :], -1.0, TPE, ALU.mult, ALU.add))
                    SH = [1, NL, E - 1]
                    own(V.tensor_tensor(ge[:, :, :], it_f[:, :].unsqueeze(2).to_broadcast(SH),
                                        base[:, 1:E].unsqueeze(1).to_broadcast(SH), ALU.is_ge))
                    own(V.tensor_tensor(gej[:, :, :], ge[:, :, :], jump[:, 0:E - 1].unsqueeze(1).to_broadcast(SH),
                                        ALU.mult))
                    own(V.tensor_reduce(sums[:, 0, :], ge[:, :, :], AX.X, ALU.add))
                    own(V.tensor_reduce(sums[:, 1, :], gej[:, :, :], AX.X, ALU.add))
                    V.tensor_copy(tile_e[:, :], sums[:, 0, :])
                    V.tensor_tensor(tile_c[:, :], sums[:, 1, :], it_f[:, :], ALU.add)
                    own(V.tensor_scalar(halves[:, :], sums[:, 0, :], 2.0, E, ALU.add, ALU.min))
                    own(V.tensor_scalar(tile_s[:, :], halves[:, :], 2.0, None, ALU.mult))
                    for h in range(2):
                        split_lo(dve, h)

        with ExitStack() as ph:
            bias = sb(ph, "bias", [P, 2 * H])
            yg = sb(ph, "yg", [P, 2, D])
            a_hi = sb(ph, "a_hi", [P, 2, D], F32R)
            a_lo = sb(ph, "a_lo", [P, 2, D], F32R)
            o_sb = sb(ph, "o_sb", [P, 2, H])
            idx_g = sb(ph, "idx_g", [P, 2], U32)
            idx_s = sb(ph, "idx_s", [P, 2], U32)
            psT = [pb(ph, f"psT2{i}", [P, D]) for i in range(2)]
            psO = [pb(ph, f"psO{i}", [P, H]) for i in range(2)]

            s_bias = sem("s_bias")
            s_yg = [sem(f"s_yg{i}") for i in range(2)]
            s_ixg = sem("s_ixg")
            s_ixs = sem("s_ixs")
            s_tr = sem("s_tr")
            s_ahi = sem("s_ahi")
            s_alo = sem("s_alo")
            s_mm = sem("s_mm")
            s_bo = sem("s_bo")
            s_out = sem("s_out")
            s_add = sem("s_add")

            def always(t, do):
                do()

            def guard(eng):
                n = eng.value_load(tiles_n[0:1, 0:1], min_val=SURE, max_val=NT)

                def there(t, do):
                    with eng.If(n > t):
                        do()
                return there

            with nc.Block() as block:

                @block.sync
                def _(sp):
                    def load_bias(e):
                        sp.wait_ge(s_split, e * KD + 1)
                        sp.sem_inc(s_sp, 1)
                        sp.dma_start(bias[:, bass.ds((e % 2) * H, H)],
                                     exp_b[bass.ds(e, 1), :].rearrange("o h -> (o h)").partition_broadcast(P)
                                     ).then_inc(s_bias, 16)

                    load_bias(0)
                    for s in range(2):
                        sp.wait_ge(s_yg[s], 16)
                    with sp.Fori(1, E, 1) as e:
                        for k in range(KD):
                            sp.wait_ge(s_split, e * KD + (k - RAW + 1))
                            sp.sem_inc(s_sp, 1)
                            load_chunk(sp, e * D + k * P, k)
                        load_bias(e)
                    sp.wait_ge(s_bias, 16 * E)

                @block.gpsimd
                def _(pool):
                    def gather(t, slot):
                        c = pool.value_load(tile_c[0:1, bass.ds(t, 1)], min_val=0, max_val=ACOLS - 1)
                        nc.gpsimd.tensor_copy(idx_g[:, slot:slot + 1], idx_all[:, bass.ds(c, 1)]).then_inc(s_ixg, 1)
                        pool.wait_ge(s_ixg, t + 1)
                        pool.sem_inc(s_step, 1)
                        pool.indirect_dma_start(
                            out=yg[:, slot, :], out_offset=None, in_=y_dram,
                            in_offset=bass.IndirectOffsetOnAxis(ap=idx_g[:, slot:slot + 1], axis=0)
                        ).then_inc(s_yg[slot], 16)

                    def regather(t, slot):
                        pool.wait_ge(s_tr, t - 1)
                        gather(t, slot)

                    def scatter(t, slot, first=False):
                        if not first:
                            pool.wait_ge(s_add, t * 16)
                        c = pool.value_load(tile_c[0:1, bass.ds(t, 1)], min_val=0, max_val=ACOLS - 1)
                        nc.gpsimd.tensor_copy(idx_s[:, slot:slot + 1], idx_all[:, bass.ds(c, 1)]).then_inc(s_ixs, 1)
                        pool.wait_ge(s_ixs, t + 1)
                        pool.wait_ge(s_out, t + 1)
                        pool.sem_inc(s_step, 1)
                        pool.indirect_dma_start(
                            out=out, out_offset=bass.IndirectOffsetOnAxis(ap=idx_s[:, slot:slot + 1], axis=0),
                            in_=o_sb[:, slot, :], in_offset=None, compute_op=ALU.add).then_inc(s_add, 16)

                    gather(0, 0)
                    gather(1, 1)
                    regather(2, 0)
                    scatter(0, 0, first=True)
                    with pool.Fori(0, (SURE - 4) // 2, 1) as i:
                        for j in range(2):
                            t = i * 2 + (j + 1)
                            regather(t + 2, (j + 1) % 2)
                            scatter(t, (j + 1) % 2)
                    there = guard(pool)
                    FROM = SURE - 3
                    with pool.Fori(0, (NT - FROM) // 2, 1) as i:
                        for j in range(2):
                            t = i * 2 + (FROM + j)
                            there(t + 2, lambda: regather(t + 2, (FROM + j) % 2))
                            there(t, lambda: scatter(t, (FROM + j) % 2))
                    pool.wait_ge(s_add, pool.value_load(tiles_n[0:1, 0:1], min_val=SURE, max_val=NT) * 16)

                def split_to(eng, reg, target, body):
                    with eng.While(lambda: eng.snap(reg) < target):
                        body(eng, eng.snap(reg))
                        eng.reg_add(reg, reg, 1)

                def tiles(eng, name, parts, finish, body):
                    reg = eng.alloc_register(name)
                    eng.reg_mov(reg, 2)

                    def needed(v):
                        e = eng.value_load(tile_e[0:1, bass.ds(v, 1)], min_val=0, max_val=E - 1)
                        split_to(eng, reg, eng.snap(e * 2 + 2), body)

                    def ahead(v):
                        t = eng.value_load(tile_s[0:1, bass.ds(v, 1)], min_val=0, max_val=2 * E)
                        with eng.If(eng.snap(reg) < t):
                            body(eng, eng.snap(reg))
                            eng.reg_add(reg, reg, 1)

                    parts(0, 0)
                    ahead(0)

                    def step(v, s, run, first=False):
                        run(v, lambda: parts(v, s))
                        run(v - 1, lambda: (needed(v - 1), finish(v - 1, (s + 1) % 2, first)))
                        run(v, lambda: ahead(v))

                    step(1, 1, always, first=True)
                    step(2, 0, always, first=True)
                    with eng.Fori(0, (SURE - 4) // 2, 1) as i:
                        for j in range(2):
                            step(i * 2 + (3 + j), (1 + j) % 2, always)
                    there = guard(eng)
                    FROM = SURE - 1
                    with eng.Fori(0, (NT - FROM) // 2, 1) as i:
                        for j in range(2):
                            step(i * 2 + (FROM + j), (FROM + j) % 2, there)
                    there(NT - 1, lambda: (needed(NT - 1), finish(NT - 1, (NT - 1) % 2, False)))
                    split_to(eng, reg, 2 * E, body)

                @block.tensor
                def _(pe):
                    pe.sem_inc(s_mm, 2)

                    def transposes(t, s):
                        pe.wait_ge(s_yg[s], (t // 2) * 16 + 16)
                        pe.wait_ge(s_alo, t + 1)
                        for k in range(KD):
                            last = nc.tensor.transpose(psT[s][:, k * P:(k + 1) * P], yg[:, s, k * P:(k + 1) * P],
                                                       ident[:, :])
                        last.then_inc(s_tr, 1)

                    def products(t, s):
                        e = pe.value_load(tile_e[0:1, bass.ds(t, 1)], min_val=0, max_val=E - 1)
                        slot = pe.snap((e % 2) * (2 * HALF))
                        pe.wait_ge(s_alo, t + 3)
                        pe.wait_ge(s_split, (e + 1) * KD)
                        pe.wait_ge(s_bo, t + 1)
                        for k in range(KD):
                            for a, ws in ((a_hi, (w_hi, w_lo)), (a_lo, (w_hi,))):
                                for w in ws:
                                    for h in range(NH):
                                        last = nc.tensor.matmul(
                                            psO[s][:, h * BANK:(h + 1) * BANK], a[:, s, k * P:(k + 1) * P],
                                            w[:, bass.ds(slot + (k * H + h * BANK), BANK)],
                                            start=(k == 0 and a is a_hi and w is w_hi),
                                            stop=(k == KD - 1 and a is a_lo))
                        last.then_inc(s_mm, 1)

                    def step(t, s, run):
                        run(t + 1, lambda: transposes(t + 1, (s + 1) % 2))
                        run(t, lambda: products(t, s))

                    transposes(0, 0)
                    with pe.Fori(0, (SURE - 2) // 2, 1) as i:
                        for j in range(2):
                            step(i * 2 + j, j, always)
                    there = guard(pe)
                    FROM = SURE - 2
                    with pe.Fori(0, (NT - 1 - FROM) // 2, 1) as i:
                        for j in range(2):
                            step(i * 2 + (FROM + j), (FROM + j) % 2, there)
                    there(NT - 1, lambda: products(NT - 1, (NT - 1) % 2))

                @block.scalar
                def _(act):
                    def parts(t, s):
                        act.wait_ge(s_tr, t + 1)
                        act.wait_ge(s_mm, t + 1)
                        nc.scalar.copy(a_hi[:, s, :], psT[s][:, :]).then_inc(s_ahi, 1)

                    def finish(t, s, first):
                        act.wait_ge(s_bo, t + 3)
                        nc.scalar.activation(o_sb[:, s, :], o_sb[:, s, :], ACTF.Relu, scale=0.5).then_inc(s_out, 1)

                    tiles(act, "split_a", parts, finish, split_hi)

                @block.vector
                def _(dve):
                    dve.sem_inc(s_alo, 2)
                    dve.sem_inc(s_bo, 2)

                    def parts(t, s):
                        dve.wait_ge(s_ahi, t + 1)
                        dve.wait_ge(s_mm, t + 1)
                        nc.vector.tensor_tensor(a_lo[:, s, :], psT[s][:, :], a_hi[:, s, :],
                                                ALU.subtract).then_inc(s_alo, 1)

                    def finish(t, s, first):
                        e = dve.value_load(tile_e[0:1, bass.ds(t, 1)], min_val=0, max_val=E - 1)
                        dve.wait_ge(s_bias, e * 16 + 16)
                        dve.wait_ge(s_mm, t + 3)
                        if not first:
                            dve.wait_ge(s_add, (t - 1) * 16)
                        nc.vector.tensor_tensor(o_sb[:, s, :], psO[s][:, :], bias[:, bass.ds((e % 2) * H, H)],
                                                ALU.add).then_inc(s_bo, 1)

                    tiles(dve, "split_v", parts, finish, split_lo)


_INS = ["x", "itok_B_0_15", "L0_cond_weights", "L0_ffn_W_gate", "L0_ffn_b_gate", "L0_ffn_W_e", "L0_ffn_b_e"]


def kernel(**inputs):
    import numpy as _np
    import concourse.bacc as _bacc
    from concourse import mybir as _mybir
    from concourse.bass_utils import run_bass_kernel_spmd as _run

    nc = _bacc.Bacc("TRN2", target_bir_lowering=False, num_devices=1)
    arrays, aps = {}, []
    for name in _INS:
        a = _np.ascontiguousarray(inputs[name])
        if name == "itok_B_0_15":
            a = a.reshape(1, -1)
        arrays[f"in_{name}"] = a
        aps.append(nc.dram_tensor(f"in_{name}", a.shape, _mybir.dt.from_np(a.dtype), kind="ExternalInput").ap())
    batches, channels, features = arrays["in_x"].shape
    experts = arrays["in_L0_ffn_W_e"].shape[0]
    tokens = batches * channels
    out = nc.dram_tensor("out", (tokens + P, features), F32, kind="ExternalOutput").ap()
    y_dram = nc.dram_tensor("y_rows", (tokens + P, features), F32).ap()
    table = nc.dram_tensor("slot_table", (experts * tokens, 1), U32).ap()
    build(nc, *aps, out, y_dram, table)
    r = _run(nc, [arrays], core_ids=[0])
    return r.results[0]["out"][:tokens].reshape(batches, channels, features)
```

```python
from contextlib import ExitStack

import numpy as np
import concourse.bass as bass
from concourse import mybir
from concourse.alu_op_type import AluOpType as ALU

P = 128
F32, F32R, BF16 = mybir.dt.float32, mybir.dt.float32r, mybir.dt.bfloat16
I32, U32 = mybir.dt.int32, mybir.dt.uint32
ACTF = mybir.ActivationFunctionType
AX = mybir.AxisListType
BANK = 512


class Chain:

    def __init__(self, eng, sem):
        self.eng, self.sem, self.base, self.n = eng, sem, 0, 0

    def turn(self, base):
        self.base, self.n = base, 0

    def __call__(self, ins):
        self.n += 1
        ins.then_inc(self.sem, 1)
        self.eng.wait_ge(self.sem, self.base + self.n)


def build(nc, x, itok, cond_w, gate_w, gate_b, exp_w, exp_b, out, y_dram, table):
    B, C, D = x.shape
    NCOND = cond_w.shape[0]
    E, _, H = exp_w.shape
    TOK = B * C
    PAIR = P // C
    KD = D // P
    NH = H // BANK
    NTILE = TOK // P
    G = 4
    NG = NTILE // G
    STORED = 2
    TPE = TOK // P
    NT = 2 * TOK // P + E - 1
    NL = NT + 3
    COLS = E * TPE
    ACOLS = COLS + TPE + E
    WARM = 40
    WARM_2 = 110
    LAND = 16 * 2 * G
    RAW = 4
    HALF = RAW * H
    SURE = 2 * TOK // P

    x_rows = x.rearrange("b c t -> (b c) t")
    w_rows = exp_w.rearrange("e (k p) h -> (e k p) h", p=P)

    with ExitStack() as both:
        def sb(ctx, name, shape, dt=F32):
            return ctx.enter_context(nc.sbuf_tensor(name, shape, dt))

        def pb(ctx, name, shape, dt=F32):
            return ctx.enter_context(nc.psum_tensor(name, shape, dt))

        def sem(name):
            return both.enter_context(nc.semaphore(name))

        w_hi = sb(both, "w_hi", [P, 4 * HALF], F32R)
        w_lo = sb(both, "w_lo", [P, 4 * HALF], F32R)
        ys = sb(both, "ys", [P, G, D])
        raw = sb(both, "raw", [P, RAW, H])
        rows = sb(both, "rows", [P, G, D])
        idx_g = sb(both, "idx_g", [P, 2], U32)
        ident = sb(both, "ident", [P, P])
        idx_all = sb(both, "idx_all", [P, ACOLS], U32)
        tile_e = sb(both, "tile_e", [1, NL], I32)
        tile_s = sb(both, "tile_s", [1, NL], I32)
        tiles_n = sb(both, "tiles_n", [1, 1], I32)
        filled = sb(both, "filled", [1, 1], I32)
        tile_c = sb(both, "tile_c", [1, NL], I32)

        s_raw = [sem(f"s_raw{i}") for i in range(RAW)]
        s_dve = sem("s_dve")
        s_hi = sem("s_hi")
        s_split = sem("s_split")

        s_yg = [sem(f"s_yg{i}") for i in range(2)]
        s_tab = sem("s_tab")
        s_first = sem("s_first")
        s_sc = [sem(f"s_sc{i}") for i in range(2)]
        s_ixg = sem("s_ixg")
        s_copy = [sem(f"s_copy{i}") for i in range(2)]
        s_sp = sem("s_sp")
        s_step = sem("s_step")

        def load_chunk(sp, row, k):
            sp.dma_start(raw[:, k % RAW, :], w_rows[bass.ds(row, P), :]).then_inc(s_raw[k % RAW], 16)

        def copies(sp, first, last):
            for c in range(first, last + 1):
                if c >= 2:
                    sp.wait_ge(s_copy[c % 2], c // 2 * 16)
                at = slice((G - STORED) * P, G * P) if c == 0 else \
                    slice((c - 1) * G * P, ((c - 1) * G + G - STORED) * P)
                sp.dma_start(out[at, :], x_rows[at, :]).then_inc(s_copy[c % 2], 16)

        def split_hi(act, h, src=raw):
            for k in range(RAW):
                at = (h % 4) * HALF + k * H
                act.wait_ge(s_raw[k], h * 16 + 16)
                nc.scalar.copy(w_hi[:, bass.ds(at, H)], src[:, k, :]).then_inc(s_hi, 1)

        def split_lo(dve, h, src=raw):
            for k in range(RAW):
                at = (h % 4) * HALF + k * H
                dve.wait_ge(s_raw[k], h * 16 + 16)
                dve.wait_ge(s_hi, h * RAW + (k + 1))
                nc.vector.tensor_tensor(w_lo[:, bass.ds(at, H)], src[:, k, :], w_hi[:, bass.ds(at, H)],
                                        ALU.subtract).then_inc(s_split, 1)

        def fetch(pool, slot):
            pool.indirect_dma_start(
                out=rows[:, slot, :], out_offset=None, in_=y_dram,
                in_offset=bass.IndirectOffsetOnAxis(ap=idx_g[:, slot:slot + 1], axis=0)).then_inc(s_yg[slot], 16)

        def gather(pool, t, slot):
            c = pool.value_load(tile_c[0:1, bass.ds(t, 1)], min_val=0, max_val=ACOLS - 1)
            nc.gpsimd.tensor_copy(idx_g[:, slot:slot + 1], idx_all[:, bass.ds(c, 1)]).then_inc(s_ixg, 1)
            pool.wait_ge(s_ixg, t + 1)
            pool.sem_inc(s_step, 1)
            fetch(pool, slot)

        with ExitStack() as ph:
            xs = rows
            bd = sb(ph, "bd", [P, G, P])
            cw = sb(ph, "cw", [P, NCOND, C])
            cond = sb(ph, "cond", [1, B], I32)
            wg = sb(ph, "wg", [P, KD, E])
            wg2 = sb(ph, "wg2", [P, KD, 2 * E], F32R)
            stack = sb(ph, "stack", [2 * E, E])
            LT = sb(ph, "LT", [2 * E, G * P])
            gb = sb(ph, "gb", [P, E])
            zero = raw[:, 0, :]
            warm = sb(ph, "warm", [1, 2])
            spare = raw[:, 1, 0:COLS].bitcast(U32)
            before = sb(ph, "before", [P, P], BF16)
            ones = sb(ph, "ones", [P, P], BF16)
            ones_f = sb(ph, "ones_f", [P, P])
            rev_i = sb(ph, "rev_i", [P, E], I32)
            rev = sb(ph, "rev", [P, E])
            it_i = sb(ph, "it_i", [1, NL], I32)
            it_f = sb(ph, "it_f", [1, NL])
            toks = sb(ph, "toks", [P, 2, G], U32)
            L = sb(ph, "L", [P, G, E])
            L2 = sb(ph, "L2", [P, G, E])
            eq = sb(ph, "eq", [P, G, E])
            top = sb(ph, "top", [P, G])
            w12 = sb(ph, "w12", [P, 2, G])
            oh = sb(ph, "oh", [P, 2, G, E])
            mask = sb(ph, "mask", [P, G, E], BF16)
            seen = sb(ph, "seen", [P, G + 1, E], BF16)
            picked = sb(ph, "picked", [P, 2, G, E])
            rank_f = sb(ph, "rank_f", [P, 2, G])
            rank = sb(ph, "rank", [P, 2, G], I32)
            rank_tile = sb(ph, "rank_tile", [P, 2, G], I32)
            rank_row = sb(ph, "rank_row", [P, 2, G], I32)
            col = sb(ph, "col", [P, 2, G])
            adr = sb(ph, "adr", [P, 2, 2, G], U32)
            cnt_f = sb(ph, "cnt_f", [1, E])
            cnt_i = sb(ph, "cnt_i", [1, E], I32)
            ntile_i = sb(ph, "ntile_i", [1, E], I32)
            ntile = sb(ph, "ntile", [1, E])
            prefix = sb(ph, "prefix", [1, 2, 2 * E])
            jump = sb(ph, "jump", [1, E])
            ge = sb(ph, "ge", [1, NL, E - 1])
            gej = sb(ph, "gej", [1, NL, E - 1])
            sums = sb(ph, "sums", [1, 2, NL])
            halves = sb(ph, "halves", [1, NL])

            psY = [pb(ph, f"psY{i}", [P, D]) for i in range(2)]
            psT = pb(ph, "psT", [P, KD, P])
            psG = pb(ph, "psG", [P, BANK])
            psR = pb(ph, "psR", [P, BANK])
            ranks_at, sums_at = slice(0, G * E), slice(2 * G * E, 3 * G * E)

            def turned(w, g, s=None):
                at = w[:, bass.ds((g % 2) * (G * D) + 2 * HALF, G * D)].rearrange("p (k c) -> p k c", k=KD)
                return at if s is None else at[:, :, s * P:(s + 1) * P]

            s_xin = [sem(f"s_xin{i}") for i in range(G)]
            s_xout = [sem(f"s_xout{i}") for i in range(G)]
            s_yout = [sem(f"s_yout{i}") for i in range(G)]
            s_cw = sem("s_cw")
            s_gw = sem("s_gw")
            s_fill = sem("s_fill")
            s_spare = sem("s_spare")
            s_const = sem("s_const")
            s_clr = sem("s_clr")
            s_bd0 = sem("s_bd0")
            s_bd = sem("s_bd")
            s_y = sem("s_y")
            s_yc = sem("s_yc")
            s_t = sem("s_t")
            s_thi = sem("s_thi")
            s_tc = sem("s_tc")
            s_gw2 = sem("s_gw2")
            s_g = sem("s_g")
            s_LT = sem("s_LT")
            s_u = sem("s_u")
            s_L = sem("s_L")
            s_mask = sem("s_mask")
            s_rank = sem("s_rank")
            s_rr = sem("s_rr")
            s_adr = sem("s_adr")
            s_scd = sem("s_scd")
            s_tok = sem("s_tok")
            s_early = sem("s_early")
            s_cnt = sem("s_cnt")

            with nc.Block() as block:

                @block.sync
                def _(sp):
                    def load(row, s):
                        sp.dma_start(xs[:, s, :], x_rows[bass.ds(row, P), :]).then_inc(s_xin[s], 16)

                    sp.dma_start(cond[:, :], itok).then_inc(s_cw, 16)
                    for i in range(PAIR):
                        sp.dma_start(cw[C * i:C * (i + 1), :, :],
                                     cond_w.rearrange("n c d -> c n d")).then_inc(s_cw, 16)
                    for s in range(G):
                        load(s * P, s)
                        if s == 0:
                            sp.dma_start(wg[:, :, :], gate_w.rearrange("(k p) e -> p k e", p=P)).then_inc(s_gw, 16)
                            sp.dma_start(gb[:, :], gate_b.partition_broadcast(P)).then_inc(s_gw, 16)

                    def store(g, s):
                        sp.wait_ge(s_xin[s], g * 16 + 16)
                        sp.dma_start(out[bass.ds((g * G + s) * P, P), :], xs[:, s, :]).then_inc(s_xout[s], 16)

                    def turn(g, first=False):
                        for s in range(G):
                            if s < STORED and not first:
                                store(g, G - STORED + s)
                            sp.wait_ge(s_y, (g * G + s + 1) + G)
                            if s >= G - STORED and not first:
                                sp.wait_ge(s_xout[s], g * 16)
                            sp.sem_inc(s_sp, 1)
                            load(((g + 1) * G + s) * P, s)

                    turn(0, first=True)
                    with sp.Fori(1, NG - 1, 1) as g:
                        turn(g)
                    for s in range(G - STORED, G):
                        store(NG - 1, s)
                    sp.wait_ge(s_spare, 32)
                    for k in range(RAW):
                        load_chunk(sp, k * P, k)

                    copies(sp, 0, 0)
                    sp.wait_ge(s_copy[0], 16)
                    copies(sp, 1, 1)
                    sp.wait_ge(s_t, 2 * NTILE)
                    for k in range(RAW):
                        sp.wait_ge(s_yout[k], 16 * NG)
                        sp.wait_ge(s_raw[k], 16)
                        sp.dma_start(ys[:, k, :], w_rows[bass.ds((RAW + k) * P, P), :]).then_inc(s_raw[k], 16)
                    sp.wait_ge(s_early, 1)
                    sp.wait_ge(s_sc[1], NG // 2 * LAND)
                    sp.dma_start(idx_all[:, 0:COLS], table.rearrange("(p c) o -> p (c o)", p=P)).then_inc(s_tab, 16)
                    copies(sp, 2, 3)
                    for s in range(G - STORED, G):
                        sp.wait_ge(s_xout[s], 16 * (NG - 1))

                @block.gpsimd
                def _(pool):
                    own = Chain(pool, s_clr)
                    own(nc.gpsimd.memset(ident[:, :], 0.0))
                    nc.gpsimd.memset(ones[:, :], 1.0)
                    own(nc.gpsimd.memset(ones_f[:, :], 1.0))
                    nc.gpsimd.affine_select(out=ident[:, :], in_=ident[:, :], compare_op=ALU.not_equal, fill=1.0,
                                            base=0, pattern=[[-1, P]], channel_multiplier=1)
                    own(nc.gpsimd.affine_select(out=before[:, :], in_=ones_f[:, :], compare_op=ALU.is_gt, fill=0.0,
                                                base=0, pattern=[[1, P]], channel_multiplier=-1))
                    nc.gpsimd.iota(rev_i[:, :], pattern=[[-1, E]], base=E, channel_multiplier=0)
                    own(nc.gpsimd.iota(it_i[:, :], pattern=[[1, NL]], base=0, channel_multiplier=0))
                    pool.sem_inc(s_const, 1)
                    nc.gpsimd.iota(toks[:, :, :], pattern=[[G * P, 2], [P, G]], base=0, channel_multiplier=1)
                    nc.gpsimd.iota(spare, pattern=[[0, COLS]], base=TOK, channel_multiplier=1)
                    nc.gpsimd.iota(idx_all[:, :], pattern=[[0, ACOLS]], base=TOK, channel_multiplier=1)
                    own(nc.gpsimd.memset(zero, 0.0))
                    pool.sem_inc(s_scd, 2)
                    pool.dma_start(table.rearrange("(p c) o -> p (c o)", p=P), spare).then_inc(s_fill, 16)
                    pool.wait_ge(s_fill, 16)


                    def turn(g, p, pairs, between=None):
                        pool.wait_ge(s_adr, g + 1)
                        pool.sem_inc(s_step, 1)
                        for r in range(2):
                            for s in range(G):
                                pool.indirect_dma_start(
                                    out=table, out_offset=bass.IndirectOffsetOnAxis(ap=adr[:, p, r, s:s + 1], axis=0),
                                    in_=toks[:, p, s:s + 1], in_offset=None).then_inc(s_sc[p], 16)
                                if between is not None and (r, s) == (1, 1):
                                    between()
                        if pairs is not None:
                            pool.wait_ge(s_sc[1 - p], pairs * LAND)
                            pool.sem_inc(s_scd, 1)
                            nc.gpsimd.tensor_scalar(toks[:, 1 - p, :], toks[:, 1 - p, :], 2 * G * P, None,
                                                    ALU.add).then_inc(s_tok, 1)
                            pool.wait_ge(s_tok, g)

                    turn(0, 0, None)
                    pool.dma_start(y_dram[TOK:TOK + P, :], zero).then_inc(s_spare, 16)
                    turn(1, 1, 1)
                    pool.dma_start(out[TOK:TOK + P, :], zero).then_inc(s_spare, 16)
                    with pool.Fori(1, NG // 2 - 1, 1) as i:
                        turn(i * 2, 0, i)
                        turn(i * 2 + 1, 1, i + 1)
                    turn(NG - 2, 0, NG // 2 - 1)

                    def early():
                        pool.wait_ge(s_first, 16)
                        pool.wait_ge(s_y, NTILE + G)
                        for s in range(G - STORED, G):
                            pool.wait_ge(s_xout[s], 16 * (NG - 1))
                        for s in range(G):
                            pool.wait_ge(s_yout[s], 16 * NG)
                        pool.wait_ge(s_spare, 32)
                        pool.sem_inc(s_step, 1)
                        n = pool.value_load(filled[0:1, 0:1], min_val=0, max_val=TOK)
                        with pool.If(n >= 2 * P):
                            pool.sem_inc(s_ixg, 2)
                            for slot in range(2):
                                fetch(pool, slot)

                    turn(NG - 1, 1, None, between=early)
                    pool.sem_inc(s_early, 1)

                @block.tensor
                def _(pe):
                    pe.sem_inc(s_y, G)
                    pe.sem_inc(s_g, 2)

                    def product(g, s):
                        n = g * G + s
                        pe.wait_ge(s_xin[s], g * 16 + 16)
                        pe.wait_ge(s_bd, (n + 1) * PAIR)
                        pe.wait_ge(s_yc, n + 1)
                        for h in range(D // BANK):
                            last = nc.tensor.matmul(psY[s % 2][:, h * BANK:(h + 1) * BANK], bd[:, s, :],
                                                    xs[:, s, h * BANK:(h + 1) * BANK], start=True, stop=True)
                        last.then_inc(s_y, 1)

                    def transposes(g, s):
                        n = g * G + s
                        pe.wait_ge(s_yc, n + 3)
                        for k in range(KD):
                            if k % (KD // 2) == 0:
                                pe.wait_ge(s_tc, n * 2 + (k // (KD // 2) + 1))
                            last = nc.tensor.transpose(psT[:, k, :], ys[:, s, k * P:(k + 1) * P], ident[:, :])
                            if k % (KD // 2) == KD // 2 - 1:
                                last.then_inc(s_t, 1)

                    def gate(g, part):
                        if part == 0:
                            pe.wait_ge(s_LT, g + 1)
                            pe.wait_ge(s_tc, (g * G + G + 1) * 2)
                        for k in range(part * (KD // 2), (part + 1) * (KD // 2)):
                            nc.tensor.matmul(psG[0:2 * E, :], wg2[:, k, :], turned(w_hi, g)[:, k, :],
                                             start=(k == 0), stop=False, skip_group_check=True)
                            last = nc.tensor.matmul(psG[0:E, :], wg2[:, k, 0:E], turned(w_lo, g)[:, k, :],
                                                    start=False, stop=(k == KD - 1), skip_group_check=True)
                        if part == 1:
                            last.then_inc(s_g, 1)

                    def unstack(g):
                        pe.wait_ge(s_LT, g + 2)
                        pe.wait_ge(s_rr, g + 1)
                        for s in range(G):
                            at = sums_at.start + s * E
                            last = nc.tensor.matmul(psR[:, at:at + E], LT[:, s * P:(s + 1) * P], stack[:, :],
                                                    start=True, stop=True)
                        last.then_inc(s_u, 1)

                    def ranks(g):
                        pe.wait_ge(s_mask, g + 1)
                        nc.tensor.matmul(psR[:, ranks_at], before[:, :], mask[:, :, :].rearrange("p g e -> p (g e)"),
                                         start=True, stop=False)
                        nc.tensor.matmul(psR[:, ranks_at], ones[:, :],
                                         seen[:, 0:G, :].rearrange("p g e -> p (g e)"),
                                         start=False, stop=True).then_inc(s_rank, 1)

                    def turn(g, first=False, second=False, last=False):
                        for s in range(G):
                            if not (last and s >= G - 2):
                                product(g + (s + 2) // G, (s + 2) % G)
                            if not (last and s == G - 1):
                                transposes(g + (s + 1) // G, (s + 1) % G)
                            if s in (0, 1) and not first:
                                gate(g - 1, s)
                            if s == 0 and not (first or second):
                                ranks(g - 2)
                            if s == 2 and not first:
                                unstack(g - 1)

                    pe.wait_ge(s_const, 1)

                    def warm_up(n):
                        for _ in range(n):
                            nc.tensor.matmul(psY[0][:, 0:P], ones[:, :], before[:, :], start=True, stop=True)

                    warm_up(WARM)
                    product(0, 0)
                    product(0, 1)
                    transposes(0, 0)
                    pe.wait_ge(s_gw2, 1)
                    turn(0, first=True)
                    turn(1, second=True)
                    with pe.Fori(2, NG - 1, 1) as g:
                        turn(g)
                    turn(NG - 1, last=True)
                    gate(NG - 1, 0)
                    gate(NG - 1, 1)
                    ranks(NG - 2)
                    unstack(NG - 1)
                    ranks(NG - 1)
                    nc.tensor.matmul(psG[:, 0:E], ones[:, :], seen[:, G, :], start=True, stop=True).then_inc(s_cnt, 1)
                    pe.wait_ge(s_first, 16)
                    warm_up(WARM_2)

                @block.scalar
                def _(act):
                    act.sem_inc(s_yc, 2)
                    act.sem_inc(s_LT, 1)
                    act.wait_ge(s_bd0, 1)
                    nc.scalar.activation(warm[:, :], warm[:, :], ACTF.Relu)
                    act.wait_ge(s_cw, 16 * (PAIR + 1))
                    act.wait_ge(s_bd0, 2)

                    regs = [act.alloc_register(f"cond{i}") for i in range(G * PAIR)]

                    def conditions(g):
                        act.load(regs, cond[0:1, bass.ds(g * (G * PAIR), G * PAIR)])

                    def diagonal(s):
                        for i in range(PAIR):
                            c = act.snap(regs[s * PAIR + i], min_val=0, max_val=NCOND - 1)
                            rows = slice(C * i, C * (i + 1))
                            nc.scalar.copy(bd[rows, s, C * i:C * (i + 1)],
                                           cw[rows, bass.ds(c, 1), :].rearrange("p o c -> p (o c)")).then_inc(s_bd, 1)

                    def high(g, s):
                        n = g * G + s
                        act.wait_ge(s_g, g + 1)
                        for b in range(2):
                            act.wait_ge(s_t, n * 2 + (b + 1))
                            ks = slice(b * (KD // 2), (b + 1) * (KD // 2))
                            nc.scalar.copy(turned(w_hi, g, s)[:, ks, :], psT[:, ks, :]).then_inc(s_thi, 1)

                    def logits_out(g):
                        act.wait_ge(s_g, g + 3)
                        nc.scalar.copy(LT[:, :], psG[0:2 * E, :]).then_inc(s_LT, 1)

                    def turn(g, first=False, last=False):
                        if not last:
                            conditions(g + 1)
                        for s in range(G):
                            n = g * G + s
                            act.wait_ge(s_y, n + 1 + G)
                            if not first:
                                act.wait_ge(s_yout[s], g * 16)
                            nc.scalar.copy(ys[:, s, :], psY[s % 2][:, :]).then_inc(s_yc, 1)
                            if not (first and s == 0):
                                high(g - (s == 0), (s - 1) % G)
                            act.wait_ge(s_yc, n + 3)
                            act.dma_start(y_dram[bass.ds(n * P, P), :], ys[:, s, :]).then_inc(s_yout[s], 16)
                            if s == G - 1 and not first:
                                logits_out(g - 1)
                            if not last:
                                diagonal(s)

                    conditions(0)
                    for s in range(G):
                        diagonal(s)
                    turn(0, first=True)
                    with act.Fori(1, NG - 1, 1) as g:
                        turn(g)
                    turn(NG - 1, last=True)
                    high(NG - 1, G - 1)
                    logits_out(NG - 1)
                    split_hi(act, 0)
                    act.wait_ge(s_sc[0], NG // 2 * LAND)
                    act.wait_ge(s_scd, NG)
                    act.wait_ge(s_adr, NG)
                    n = act.value_load(filled[0:1, 0:1], min_val=0, max_val=TOK)
                    with act.If(n >= 2 * P):
                        act.dma_start(idx_g[:, :],
                                      table.rearrange("(p c) o -> p (c o)", p=P)[:, 0:2]).then_inc(s_first, 16)
                    with act.If(n < 2 * P):
                        act.sem_inc(s_first, 16)
                    split_hi(act, 1, ys)
                    for s in range(G):
                        act.wait_ge(s_yout[s], 16 * NG)

                @block.vector
                def _(dve):
                    own = Chain(dve, s_dve)
                    V = nc.vector
                    V.memset(warm[:, :], 0.0).then_inc(s_bd0, 1)
                    V.memset(bd[:, :, :], 0.0).then_inc(s_bd0, 1)
                    dve.sem_inc(s_tc, 2)
                    dve.sem_inc(s_rr, 1)
                    own(V.memset(seen[:, :, :], 0.0))
                    dve.wait_ge(s_const, 1)
                    V.tensor_copy(it_f[:, :], it_i[:, :])
                    own(V.tensor_copy(rev[:, :], rev_i[:, :]))
                    dve.wait_ge(s_gw, 32)
                    GE = [P, G, E]
                    revb = rev[:, :].unsqueeze(1).to_broadcast(GE)

                    own(V.tensor_copy(wg2[:, :, 0:E], wg[:, :, :]))
                    own(V.tensor_tensor(wg2[:, :, E:2 * E], wg[:, :, :], wg2[:, :, 0:E], ALU.subtract))
                    own(V.tensor_tensor(stack[:, :], ident[0:2 * E, 0:E], ident[0:2 * E, E:2 * E], ALU.add))
                    dve.sem_inc(s_gw2, 1)

                    def low(g, s):
                        n = g * G + s
                        dve.wait_ge(s_g, g + 1)
                        for b in range(2):
                            ks = slice(b * (KD // 2), (b + 1) * (KD // 2))
                            dve.wait_ge(s_thi, n * 2 + (b + 1))
                            V.tensor_tensor(turned(w_lo, g, s)[:, ks, :], psT[:, ks, :],
                                            turned(w_hi, g, s)[:, ks, :], ALU.subtract).then_inc(s_tc, 1)

                    def logits(g):
                        dve.wait_ge(s_u, g + 1)
                        V.tensor_tensor(L[:, :, :], psR[:, sums_at].rearrange("p (g e) -> p g e", e=E),
                                        gb[:, :].unsqueeze(1).to_broadcast(GE), ALU.add).then_inc(s_L, 1)

                    def choose(g, r):
                        if r == 0:
                            dve.wait_ge(s_L, g + 1)
                        src = (L, L2)[r]
                        own(V.tensor_reduce(top[:, :], src[:, :, :], AX.X, ALU.max))
                        own(V.tensor_tensor(eq[:, :, :], src[:, :, :],
                                            top[:, :].unsqueeze(2).to_broadcast(GE), ALU.is_ge))
                        own(V.tensor_tensor(eq[:, :, :], eq[:, :, :], revb, ALU.mult))
                        own(V.tensor_reduce(w12[:, r, :], eq[:, :, :], AX.X, ALU.max))
                        own(V.tensor_tensor(oh[:, r, :, :], w12[:, r, :].unsqueeze(2).to_broadcast(GE), revb,
                                            ALU.is_equal))
                        if r == 0:
                            own(V.scalar_tensor_tensor(L2[:, :, :], oh[:, 0, :, :], -3.0e38, L[:, :, :],
                                                       ALU.mult, ALU.add))

                    def masks():
                        own(V.tensor_tensor(mask[:, :, :], oh[:, 0, :, :], oh[:, 1, :, :], ALU.add))
                        own(V.tensor_copy(seen[:, 0, :], seen[:, G, :]))
                        for s in range(G):
                            own(V.tensor_tensor(seen[:, s + 1, :], seen[:, s, :], mask[:, s, :], ALU.add))
                        dve.sem_inc(s_mask, 1)

                    def slots(g, last=False):
                        dve.wait_ge(s_rank, g + 1)
                        if last:
                            own(V.tensor_copy(filled[:, :], psR[0:1, 0:1]))
                        own(V.tensor_tensor(picked[:, :, :, :], oh[:, :, :, :],
                                            psR[:, ranks_at].rearrange("p (g e) -> p g e", e=E).unsqueeze(1)
                                            .to_broadcast([P, 2, G, E]), ALU.mult))
                        dve.sem_inc(s_rr, 1)
                        own(V.tensor_reduce(rank_f[:, :, :], picked[:, :, :, :], AX.X, ALU.add))
                        own(V.tensor_copy(rank[:, :, :], rank_f[:, :, :]))
                        V.tensor_scalar(rank_tile[:, :, :], rank[:, :, :], 7, None, ALU.logical_shift_right)
                        V.tensor_scalar(rank_row[:, :, :], rank[:, :, :], P - 1, None, ALU.bitwise_and)
                        own(V.tensor_scalar(col[:, :, :], w12[:, :, :], -TPE, E * TPE, ALU.mult, ALU.add))
                        own(V.tensor_tensor(col[:, :, :], col[:, :, :], rank_tile[:, :, :], ALU.add))
                        dve.wait_ge(s_scd, g + 1)
                        own(V.scalar_tensor_tensor(adr[:, bass.ds(g % 2, 1), :, :].rearrange("p o r s -> p (o r) s"),
                                                   rank_row[:, :, :], COLS, col[:, :, :],
                                                   ALU.mult, ALU.add))
                        dve.sem_inc(s_adr, 1)

                    def turn(g, second=False, last=False):
                        low(g, 1)
                        if not second:
                            slots(g - 2)
                        low(g, 2)
                        low(g, 3)
                        logits(g - 1)
                        choose(g - 1, 0)
                        if not last:
                            low(g + 1, 0)
                        choose(g - 1, 1)
                        masks()
                        if last:
                            slots(g - 1)

                    for s in range(G + 1):
                        low(s // G, s % G)
                    turn(1, second=True)
                    start = own.n
                    STEPS = 11 + 2 + G + 6
                    with dve.Fori(2, NG - 1, 1) as g:
                        own.turn((g - 2) * STEPS + start)
                        turn(g)
                        assert own.n == STEPS, own.n
                    own.turn((NG - 3) * STEPS + start)
                    turn(NG - 1, last=True)
                    logits(NG - 1)
                    choose(NG - 1, 0)
                    choose(NG - 1, 1)
                    masks()
                    slots(NG - 1, last=True)
                    dve.wait_ge(s_cnt, 1)
                    own(V.tensor_scalar(cnt_f[:, :], psG[0:1, 0:E], P - 1, None, ALU.add))
                    own(V.tensor_copy(cnt_i[:, :], cnt_f[:, :]))
                    own(V.tensor_scalar(ntile_i[:, :], cnt_i[:, :], 7, None, ALU.logical_shift_right))
                    V.tensor_copy(ntile[:, :], ntile_i[:, :])
                    own(V.memset(prefix[:, :, :], 0.0))
                    own(V.tensor_copy(prefix[:, 0, E:2 * E], ntile[:, :]))
                    dist, side = 1, 0
                    while dist < E:
                        own(V.tensor_tensor(prefix[:, 1 - side, E:2 * E], prefix[:, side, E:2 * E],
                                            prefix[:, side, E - dist:2 * E - dist], ALU.add))
                        dist, side = dist * 2, 1 - side
                    base = prefix[:, side, E - 1:2 * E]
                    V.tensor_copy(tiles_n[:, :], base[:, E:E + 1])
                    own(V.tensor_scalar(jump[:, :], ntile[:, :], -1.0, TPE, ALU.mult, ALU.add))
                    SH = [1, NL, E - 1]
                    own(V.tensor_tensor(ge[:, :, :], it_f[:, :].unsqueeze(2).to_broadcast(SH),
                                        base[:, 1:E].unsqueeze(1).to_broadcast(SH), ALU.is_ge))
                    own(V.tensor_tensor(gej[:, :, :], ge[:, :, :], jump[:, 0:E - 1].unsqueeze(1).to_broadcast(SH),
                                        ALU.mult))
                    own(V.tensor_reduce(sums[:, 0, :], ge[:, :, :], AX.X, ALU.add))
                    own(V.tensor_reduce(sums[:, 1, :], gej[:, :, :], AX.X, ALU.add))
                    V.tensor_copy(tile_e[:, :], sums[:, 0, :])
                    V.tensor_tensor(tile_c[:, :], sums[:, 1, :], it_f[:, :], ALU.add)
                    own(V.tensor_scalar(halves[:, :], sums[:, 0, :], 2.0, E, ALU.add, ALU.min))
                    own(V.tensor_scalar(tile_s[:, :], halves[:, :], 2.0, None, ALU.mult))
                    split_lo(dve, 0)

        with ExitStack() as ph:
            bias = sb(ph, "bias", [P, 2 * H])
            yg = rows[:, 0:2, :]
            a_hi = sb(ph, "a_hi", [P, 2, D], F32R)
            a_lo = sb(ph, "a_lo", [P, 2, D], F32R)
            o_sb = rows[:, 2:4, :]
            idx_s = sb(ph, "idx_s", [P, 2], U32)
            psT = [pb(ph, f"psT2{i}", [P, D]) for i in range(2)]
            psO = [pb(ph, f"psO{i}", [P, H]) for i in range(2)]

            s_bias = sem("s_bias")
            s_ixs = sem("s_ixs")
            s_tr = sem("s_tr")
            s_ahi = sem("s_ahi")
            s_alo = sem("s_alo")
            s_mm = sem("s_mm")
            s_bo = sem("s_bo")
            s_out = sem("s_out")
            s_add = sem("s_add")

            def always(t, do):
                do()

            def guard(eng):
                n = eng.value_load(tiles_n[0:1, 0:1], min_val=SURE, max_val=NT)

                def there(t, do):
                    with eng.If(n > t):
                        do()
                return there

            with nc.Block() as block:

                @block.sync
                def _(sp):
                    def load_bias(e):
                        sp.wait_ge(s_split, e * KD + 1)
                        sp.sem_inc(s_sp, 1)
                        sp.dma_start(bias[:, bass.ds((e % 2) * H, H)],
                                     exp_b[bass.ds(e, 1), :].rearrange("o h -> (o h)").partition_broadcast(P)
                                     ).then_inc(s_bias, 16)

                    load_bias(0)
                    copies(sp, 4, NG)
                    for s in range(2):
                        sp.wait_ge(s_yg[s], 16)
                    with sp.Fori(1, E, 1) as e:
                        for k in range(KD):
                            sp.wait_ge(s_split, e * KD + (k - RAW + 1))
                            sp.sem_inc(s_sp, 1)
                            load_chunk(sp, e * D + k * P, k)
                        load_bias(e)
                    sp.wait_ge(s_bias, 16 * E)

                @block.gpsimd
                def _(pool):
                    def regather(t, slot):
                        pool.wait_ge(s_tr, t - 1)
                        gather(pool, t, slot)

                    def scatter(t, slot, first=False):
                        if not first:
                            pool.wait_ge(s_add, t * 16)
                        c = pool.value_load(tile_c[0:1, bass.ds(t, 1)], min_val=0, max_val=ACOLS - 1)
                        nc.gpsimd.tensor_copy(idx_s[:, slot:slot + 1], idx_all[:, bass.ds(c, 1)]).then_inc(s_ixs, 1)
                        pool.wait_ge(s_ixs, t + 1)
                        pool.wait_ge(s_out, t + 1)
                        pool.sem_inc(s_step, 1)
                        pool.indirect_dma_start(
                            out=out, out_offset=bass.IndirectOffsetOnAxis(ap=idx_s[:, slot:slot + 1], axis=0),
                            in_=o_sb[:, slot, :], in_offset=None, compute_op=ALU.add).then_inc(s_add, 16)

                    pool.wait_ge(s_tab, 16)
                    n = pool.value_load(filled[0:1, 0:1], min_val=0, max_val=TOK)
                    with pool.If(n < 2 * P):
                        gather(pool, 0, 0)
                        gather(pool, 1, 1)
                    regather(2, 0)
                    regather(3, 1)
                    for j in range(2):
                        pool.wait_ge(s_copy[j], (NG // 2 + 1 - j) * 16)
                    scatter(0, 0, first=True)
                    with pool.Fori(0, (SURE - 4) // 2, 1) as i:
                        for j in range(2):
                            t = i * 2 + (j + 1)
                            regather(t + 3, j)
                            scatter(t, (j + 1) % 2)
                    there = guard(pool)
                    FROM = SURE - 3
                    with pool.Fori(0, (NT - FROM) // 2, 1) as i:
                        for j in range(2):
                            t = i * 2 + (FROM + j)
                            there(t + 3, lambda: regather(t + 3, (FROM + 1 + j) % 2))
                            there(t, lambda: scatter(t, (FROM + j) % 2))
                    pool.wait_ge(s_add, pool.value_load(tiles_n[0:1, 0:1], min_val=SURE, max_val=NT) * 16)

                def split_to(eng, reg, target, body):
                    with eng.While(lambda: eng.snap(reg) < target):
                        body(eng, eng.snap(reg))
                        eng.reg_add(reg, reg, 1)

                def tiles(eng, name, parts, finish, body, begin=lambda: None):
                    reg = eng.alloc_register(name)
                    eng.reg_mov(reg, 2)

                    def needed(v):
                        e = eng.value_load(tile_e[0:1, bass.ds(v, 1)], min_val=0, max_val=E - 1)
                        split_to(eng, reg, eng.snap(e * 2 + 2), body)

                    def ahead(v):
                        t = eng.value_load(tile_s[0:1, bass.ds(v, 1)], min_val=0, max_val=2 * E)
                        with eng.If(eng.snap(reg) < t):
                            body(eng, eng.snap(reg))
                            eng.reg_add(reg, reg, 1)

                    parts(0, 0)
                    begin()

                    def step(v, s, run, first=False, ahead_too=True):
                        run(v, lambda: parts(v, s))
                        run(v - 1, lambda: (needed(v - 1), finish(v - 1, (s + 1) % 2, first)))
                        if ahead_too:
                            run(v, lambda: ahead(v))

                    step(1, 1, always, first=True, ahead_too=False)
                    step(2, 0, always, first=True)
                    with eng.Fori(0, (SURE - 4) // 2, 1) as i:
                        for j in range(2):
                            step(i * 2 + (3 + j), (1 + j) % 2, always)
                    there = guard(eng)
                    FROM = SURE - 1
                    with eng.Fori(0, (NT - FROM) // 2, 1) as i:
                        for j in range(2):
                            step(i * 2 + (FROM + j), (FROM + j) % 2, there)
                    there(NT - 1, lambda: (needed(NT - 1), finish(NT - 1, (NT - 1) % 2, False)))
                    split_to(eng, reg, 2 * E, body)

                @block.tensor
                def _(pe):
                    pe.sem_inc(s_mm, 2)

                    def transposes(t, s):
                        pe.wait_ge(s_yg[s], (t // 2) * 16 + 16)
                        pe.wait_ge(s_alo, t + 1)
                        for k in range(KD):
                            last = nc.tensor.transpose(psT[s][:, k * P:(k + 1) * P], yg[:, s, k * P:(k + 1) * P],
                                                       ident[:, :])
                        last.then_inc(s_tr, 1)

                    def products(t, s):
                        e = pe.value_load(tile_e[0:1, bass.ds(t, 1)], min_val=0, max_val=E - 1)
                        slot = pe.snap((e % 2) * (2 * HALF))
                        pe.wait_ge(s_alo, t + 3)
                        pe.wait_ge(s_split, e * KD + RAW)
                        pe.wait_ge(s_bo, t + 1)
                        for k in range(KD):
                            if k == RAW:
                                pe.wait_ge(s_split, (e + 1) * KD)
                            for a, ws in ((a_hi, (w_hi, w_lo)), (a_lo, (w_hi,))):
                                for w in ws:
                                    for h in range(NH):
                                        last = nc.tensor.matmul(
                                            psO[s][:, h * BANK:(h + 1) * BANK], a[:, s, k * P:(k + 1) * P],
                                            w[:, bass.ds(slot + (k * H + h * BANK), BANK)],
                                            start=(k == 0 and a is a_hi and w is w_hi),
                                            stop=(k == KD - 1 and a is a_lo))
                        last.then_inc(s_mm, 1)

                    def step(t, s, run):
                        run(t + 1, lambda: transposes(t + 1, (s + 1) % 2))
                        run(t, lambda: products(t, s))

                    transposes(0, 0)
                    with pe.Fori(0, (SURE - 2) // 2, 1) as i:
                        for j in range(2):
                            step(i * 2 + j, j, always)
                    there = guard(pe)
                    FROM = SURE - 2
                    with pe.Fori(0, (NT - 1 - FROM) // 2, 1) as i:
                        for j in range(2):
                            step(i * 2 + (FROM + j), (FROM + j) % 2, there)
                    there(NT - 1, lambda: products(NT - 1, (NT - 1) % 2))

                @block.scalar
                def _(act):
                    def parts(t, s):
                        act.wait_ge(s_tr, t + 1)
                        act.wait_ge(s_mm, t + 1)
                        nc.scalar.copy(a_hi[:, s, :], psT[s][:, :]).then_inc(s_ahi, 1)

                    def finish(t, s, first):
                        act.wait_ge(s_bo, t + 3)
                        nc.scalar.activation(o_sb[:, s, :], o_sb[:, s, :], ACTF.Relu, scale=0.5).then_inc(s_out, 1)

                    tiles(act, "split_a", parts, finish, split_hi)

                @block.vector
                def _(dve):
                    dve.sem_inc(s_alo, 2)
                    dve.sem_inc(s_bo, 2)

                    def parts(t, s):
                        dve.wait_ge(s_ahi, t + 1)
                        dve.wait_ge(s_mm, t + 1)
                        nc.vector.tensor_tensor(a_lo[:, s, :], psT[s][:, :], a_hi[:, s, :],
                                                ALU.subtract).then_inc(s_alo, 1)

                    def finish(t, s, first):
                        e = dve.value_load(tile_e[0:1, bass.ds(t, 1)], min_val=0, max_val=E - 1)
                        dve.wait_ge(s_bias, e * 16 + 16)
                        dve.wait_ge(s_mm, t + 3)
                        if not first:
                            dve.wait_ge(s_add, (t - 1) * 16)
                        nc.vector.tensor_tensor(o_sb[:, s, :], psO[s][:, :], bias[:, bass.ds((e % 2) * H, H)],
                                                ALU.add).then_inc(s_bo, 1)

                    tiles(dve, "split_v", parts, finish, split_lo, begin=lambda: split_lo(dve, 1, ys))


_INS = ["x", "itok_B_0_15", "L0_cond_weights", "L0_ffn_W_gate", "L0_ffn_b_gate", "L0_ffn_W_e", "L0_ffn_b_e"]


def kernel(**inputs):
    import numpy as _np
    import concourse.bacc as _bacc
    from concourse import mybir as _mybir
    from concourse.bass_utils import run_bass_kernel_spmd as _run

    nc = _bacc.Bacc("TRN2", target_bir_lowering=False, num_devices=1)
    arrays, aps = {}, []
    for name in _INS:
        a = _np.ascontiguousarray(inputs[name])
        if name == "itok_B_0_15":
            a = a.reshape(1, -1)
        arrays[f"in_{name}"] = a
        aps.append(nc.dram_tensor(f"in_{name}", a.shape, _mybir.dt.from_np(a.dtype), kind="ExternalInput").ap())
    batches, channels, features = arrays["in_x"].shape
    experts = arrays["in_L0_ffn_W_e"].shape[0]
    tokens = batches * channels
    out = nc.dram_tensor("out", (tokens + P, features), F32, kind="ExternalOutput").ap()
    y_dram = nc.dram_tensor("y_rows", (tokens + P, features), F32).ap()
    table = nc.dram_tensor("slot_table", (experts * tokens, 1), U32).ap()
    build(nc, *aps, out, y_dram, table)
    r = _run(nc, [arrays], core_ids=[0])
    return r.results[0]["out"][:tokens].reshape(batches, channels, features)
```
